# Optimizing a Trainium2 kernel written in Bass

```python
import numpy as np
import jax
import jax.numpy as jnp

def _softmax(x, axis=-1):
    return jax.nn.softmax(x, axis=axis)
def _gelu(x):
    return jax.nn.gelu(x, approximate=True)
def _silu(x):
    return jax.nn.silu(x)
def _sigmoid(x):
    return jax.nn.sigmoid(x)
def _layernorm(x, axis=-1, eps=1e-5):
    m = jnp.mean(x, axis=axis, keepdims=True)
    v = jnp.var(x, axis=axis, keepdims=True)
    return (x - m) / jnp.sqrt(v + eps)
def _scatter_add(tgt, idx, src, axis=0):
    return tgt.at[idx].add(src)
def _segment_sum(src, seg, n):
    return jax.ops.segment_sum(src, seg, n)

kernel_name = 'mk_conv_preact_d4_conv_nhwc128_46fb7a'

def setup_inputs(seed: int = 0):
    np.random.seed(seed)
    _w = jnp.asarray
    def _rec_inputs():
        import jax
        import jax.numpy as jnp
        _gk = jax.random.key(seed)
        x = 7.22e-05 + 1 * jax.random.normal(jax.random.fold_in(_gk, 1), (16, 64, 64, 128), jnp.float32)
        return x
    x = _rec_inputs()
    def _L0_conv_setup():
        import jax, jax.numpy as jnp
        import numpy as np
        HEADS = 4
        DIM_HEAD = 32
        EPS = 1e-05
        key = jax.random.key(seed)
        ks = jax.random.split(key, 3)
        B, H, W, C = (16, 64, 64, 128)
        hidden = HEADS * DIM_HEAD
        x = jax.random.normal(ks[0], (B, H, W, C), dtype=jnp.float32)
        w_qkv = jax.random.normal(ks[1], (C, 3 * hidden), dtype=jnp.float32) * 0.05
        w_out = jax.random.normal(ks[2], (hidden, C), dtype=jnp.float32) * 0.05
        b_out = jnp.zeros((C,), dtype=jnp.float32)
        g_ln = jnp.ones((C,), dtype=jnp.float32)
        b_ln = jnp.zeros((C,), dtype=jnp.float32)
        return {'x': x, 'w_qkv': w_qkv, 'w_out': w_out, 'b_out': b_out, 'g_ln': g_ln, 'b_ln': b_ln}
    _L0_conv_all = _L0_conv_setup()
    _L0_conv_in = {k: v for k, v in _L0_conv_all.items() if k in ('w_qkv', 'w_out', 'b_out', 'g_ln', 'b_ln', )}
    del _L0_conv_all

    def _L1_conv_setup():
        import jax, jax.numpy as jnp
        import numpy as np
        LN_EPS = 1e-05

        def _layer_norm(h, g, b):
            mu = jnp.mean(h, axis=-1, keepdims=True)
            var = jnp.mean(jnp.square(h - mu), axis=-1, keepdims=True)
            return (h - mu) * jax.lax.rsqrt(var + LN_EPS) * g + b

        def _forward_fourier(x, w1, w2):
            xt = jnp.transpose(x, (0, 3, 1, 2))
            B, I, M, N = xt.shape
            nm = w1.shape[2]
            cw1 = w1[..., 0] + 1j * w1[..., 1]
            cw2 = w2[..., 0] + 1j * w2[..., 1]
            O = cw1.shape[1]
            fty = jnp.fft.rfft(xt, axis=-1, norm='ortho')
            f1 = jnp.einsum('bixy,ioy->boxy', fty[..., :nm], cw1)
            pad_y = jnp.zeros((B, O, M, N // 2 + 1 - nm), dtype=f1.dtype)
            xy = jnp.fft.irfft(jnp.concatenate([f1, pad_y], axis=-1), n=N, axis=-1, norm='ortho')
            ftx = jnp.fft.rfft(xt, axis=-2, norm='ortho')
            f2 = jnp.einsum('bixy,iox->boxy', ftx[:, :, :nm, :], cw2)
            pad_x = jnp.zeros((B, O, M // 2 + 1 - nm, N), dtype=f2.dtype)
            xx = jnp.fft.irfft(jnp.concatenate([f2, pad_x], axis=-2), n=M, axis=-2, norm='ortho')
            return jnp.transpose(xx + xy, (0, 2, 3, 1))
        key = jax.random.key(seed)
        ks = jax.random.split(key, 6)
        B, M, N, D = (16, 128, 128, 128)
        NM, H = (16, 512)
        xav = float(np.sqrt(2.0 / (D + D)))
        return {'x': jax.random.normal(ks[0], (B, M, N, D), jnp.float32), 'w1': jax.random.normal(ks[1], (D, D, NM, 2), jnp.float32) * xav, 'w2': jax.random.normal(ks[2], (D, D, NM, 2), jnp.float32) * xav, 'ff_w0': jax.random.normal(ks[3], (D, H), jnp.float32) * float(1.0 / np.sqrt(D)), 'ff_b0': jnp.zeros((H,), jnp.float32), 'ff_w1': jax.random.normal(ks[4], (H, D), jnp.float32) * float(1.0 / np.sqrt(H)), 'ff_b1': jnp.zeros((D,), jnp.float32), 'ln_g': jnp.ones((D,), jnp.float32), 'ln_b': jnp.zeros((D,), jnp.float32)}
    _L1_conv_all = _L1_conv_setup()
    _L1_conv_in = {k: v for k, v in _L1_conv_all.items() if k in ('w1', 'w2', 'ff_w0', 'ff_b0', 'ff_w1', 'ff_b1', 'ln_g', 'ln_b', )}
    del _L1_conv_all

    def _L2_conv_setup():
        import jax, jax.numpy as jnp
        import numpy as np
        from jax import lax
        B, H, W, C = (4, 48, 48, 128)
        D_INNER, D_STATE, DT_RANK, K = (256, 16, 8, 4)
        key = jax.random.key(seed)
        ks = jax.random.split(key, 8)
        d, N, R = (D_INNER, D_STATE, DT_RANK)
        f32 = jnp.float32
        return {'x': jax.random.normal(ks[0], (B, H, W, C), f32), 'in_proj_w': jax.random.normal(ks[1], (2 * d, C), f32) * C ** (-0.5), 'conv_w': jax.random.normal(ks[2], (d, 1, 3, 3), f32) / 3.0, 'conv_b': jnp.zeros((d,), f32), 'x_proj_w': jax.random.normal(ks[3], (K, R + 2 * N, d), f32) * d ** (-0.5), 'dt_proj_w': jax.random.normal(ks[4], (K, d, R), f32) * R ** (-0.5), 'dt_proj_b': jax.random.uniform(ks[5], (K, d), f32, -4.0, -2.0), 'A_logs': jnp.broadcast_to(jnp.log(jnp.arange(1, N + 1, dtype=f32)), (K * d, N)).copy(), 'Ds': jnp.ones((K * d,), f32), 'norm_g': jnp.ones((d,), f32), 'norm_b': jnp.zeros((d,), f32), 'out_proj_w': jax.random.normal(ks[6], (C, d), f32) * d ** (-0.5)}
    _L2_conv_all = _L2_conv_setup()
    _L2_conv_in = {k: v for k, v in _L2_conv_all.items() if k in ('in_proj_w', 'conv_w', 'conv_b', 'x_proj_w', 'dt_proj_w', 'dt_proj_b', 'A_logs', 'Ds', 'norm_g', 'norm_b', 'out_proj_w', )}
    del _L2_conv_all

    def _L3_conv_setup():
        import jax, jax.numpy as jnp
        import numpy as np
        D_STATE = 8
        DT_RANK = 8

        def _grouped_1x1(x, w):
            B, H, W, _ = x.shape
            g, o, i = w.shape
            xg = x.reshape(B, H, W, g, i)
            return jnp.einsum('bhwgi,goi->bhwgo', xg, w).reshape(B, H, W, g * o)

        def _mamba(x_seq, in_proj_w, conv1d_w, conv1d_b, x_proj_w, dt_proj_w, dt_proj_b, A_log, D_param, out_proj_w):
            B, L, D = x_seq.shape
            N, R = (D_STATE, DT_RANK)
            xz = jnp.einsum('bld,ed->ble', x_seq, in_proj_w)
            u, z = (xz[..., :D], xz[..., D:])
            up = jnp.pad(u, ((0, 0), (2, 0), (0, 0)))
            u = up[:, 0:L] * conv1d_w[:, 0] + up[:, 1:L + 1] * conv1d_w[:, 1] + up[:, 2:L + 2] * conv1d_w[:, 2] + conv1d_b
            u = jax.nn.silu(u)
            x_dbl = jnp.einsum('bld,ed->ble', u, x_proj_w)
            dt = x_dbl[..., :R]
            Bm = x_dbl[..., R:R + N]
            Cm = x_dbl[..., R + N:]
            delta = jax.nn.softplus(jnp.einsum('blr,dr->bld', dt, dt_proj_w) + dt_proj_b)
            A = -jnp.exp(A_log)

            def step(h, inp):
                d_t, u_t, b_t, c_t = inp
                dA = jnp.exp(d_t[..., None] * A)
                h = dA * h + (d_t * u_t)[..., None] * b_t[:, None, :]
                y_t = jnp.einsum('bdn,bn->bd', h, c_t)
                return (h, y_t)
            h0 = jnp.zeros((B, D, N), dtype=x_seq.dtype)
            xs = (jnp.swapaxes(delta, 0, 1), jnp.swapaxes(u, 0, 1), jnp.swapaxes(Bm, 0, 1), jnp.swapaxes(Cm, 0, 1))
            _, ys = jax.lax.scan(step, h0, xs)
            y = jnp.swapaxes(ys, 0, 1) + u * D_param
            y = y * jax.nn.silu(z)
            return jnp.einsum('bld,ed->ble', y, out_proj_w)
        key = jax.random.key(seed)
        ks = jax.random.split(key, 16)
        B, H, W, C = (8, 64, 64, 128)
        g = 4
        D = 128
        N = D_STATE
        R = DT_RANK
        inp = {}
        inp['x'] = jax.random.normal(ks[0], (B, H, W, C), dtype=jnp.float32)
        inp['w1'] = jax.random.normal(ks[1], (g, D // g, C // g), dtype=jnp.float32) * 0.1
        inp['dw'] = jax.random.normal(ks[2], (3, 3, 1, D), dtype=jnp.float32) * 0.1
        inp['in_proj_w'] = jax.random.normal(ks[3], (2 * D, D), dtype=jnp.float32) * 0.05
        inp['conv1d_w'] = jax.random.normal(ks[4], (D, 3), dtype=jnp.float32) * 0.1
        inp['conv1d_b'] = jax.random.normal(ks[5], (D,), dtype=jnp.float32) * 0.05
        inp['x_proj_w'] = jax.random.normal(ks[6], (R + 2 * N, D), dtype=jnp.float32) * 0.05
        inp['dt_proj_w'] = jax.random.normal(ks[7], (D, R), dtype=jnp.float32) * 0.05
        inp['dt_proj_b'] = jax.random.normal(ks[8], (D,), dtype=jnp.float32) * 0.05
        inp['A_log'] = jnp.log(jnp.tile(jnp.arange(1, N + 1, dtype=jnp.float32)[None, :], (D, 1)))
        inp['D_param'] = jnp.ones((D,), dtype=jnp.float32)
        inp['out_proj_w'] = jax.random.normal(ks[9], (D, D), dtype=jnp.float32) * 0.05
        inp['gamma'] = jnp.ones((D,), dtype=jnp.float32)
        inp['beta'] = jnp.zeros((D,), dtype=jnp.float32)
        inp['w2'] = jax.random.normal(ks[10], (g, D // g, C // g), dtype=jnp.float32) * 0.1
        inp['wout'] = jax.random.normal(ks[11], (g, C // g, D // g), dtype=jnp.float32) * 0.1
        return inp
    _L3_conv_all = _L3_conv_setup()
    _L3_conv_in = {k: v for k, v in _L3_conv_all.items() if k in ('w1', 'dw', 'in_proj_w', 'conv1d_w', 'conv1d_b', 'x_proj_w', 'dt_proj_w', 'dt_proj_b', 'A_log', 'D_param', 'out_proj_w', 'gamma', 'beta', 'w2', 'wout', )}
    del _L3_conv_all

    return {
        "x": x,
        "L0_conv_w_qkv": _L0_conv_in["w_qkv"],
        "L0_conv_w_out": _L0_conv_in["w_out"],
        "L0_conv_b_out": _L0_conv_in["b_out"],
        "L0_conv_g_ln": _L0_conv_in["g_ln"],
        "L0_conv_b_ln": _L0_conv_in["b_ln"],
        "L1_conv_w1": _L1_conv_in["w1"],
        "L1_conv_w2": _L1_conv_in["w2"],
        "L1_conv_ff_w0": _L1_conv_in["ff_w0"],
        "L1_conv_ff_b0": _L1_conv_in["ff_b0"],
        "L1_conv_ff_w1": _L1_conv_in["ff_w1"],
        "L1_conv_ff_b1": _L1_conv_in["ff_b1"],
        "L1_conv_ln_g": _L1_conv_in["ln_g"],
        "L1_conv_ln_b": _L1_conv_in["ln_b"],
        "L2_conv_in_proj_w": _L2_conv_in["in_proj_w"],
        "L2_conv_conv_w": _L2_conv_in["conv_w"],
        "L2_conv_conv_b": _L2_conv_in["conv_b"],
        "L2_conv_x_proj_w": _L2_conv_in["x_proj_w"],
        "L2_conv_dt_proj_w": _L2_conv_in["dt_proj_w"],
        "L2_conv_dt_proj_b": _L2_conv_in["dt_proj_b"],
        "L2_conv_A_logs": _L2_conv_in["A_logs"],
        "L2_conv_Ds": _L2_conv_in["Ds"],
        "L2_conv_norm_g": _L2_conv_in["norm_g"],
        "L2_conv_norm_b": _L2_conv_in["norm_b"],
        "L2_conv_out_proj_w": _L2_conv_in["out_proj_w"],
        "L3_conv_w1": _L3_conv_in["w1"],
        "L3_conv_dw": _L3_conv_in["dw"],
        "L3_conv_in_proj_w": _L3_conv_in["in_proj_w"],
        "L3_conv_conv1d_w": _L3_conv_in["conv1d_w"],
        "L3_conv_conv1d_b": _L3_conv_in["conv1d_b"],
        "L3_conv_x_proj_w": _L3_conv_in["x_proj_w"],
        "L3_conv_dt_proj_w": _L3_conv_in["dt_proj_w"],
        "L3_conv_dt_proj_b": _L3_conv_in["dt_proj_b"],
        "L3_conv_A_log": _L3_conv_in["A_log"],
        "L3_conv_D_param": _L3_conv_in["D_param"],
        "L3_conv_out_proj_w": _L3_conv_in["out_proj_w"],
        "L3_conv_gamma": _L3_conv_in["gamma"],
        "L3_conv_beta": _L3_conv_in["beta"],
        "L3_conv_w2": _L3_conv_in["w2"],
        "L3_conv_wout": _L3_conv_in["wout"],
    }

def reference(x, L0_conv_w_qkv, L0_conv_w_out, L0_conv_b_out, L0_conv_g_ln, L0_conv_b_ln, L1_conv_w1, L1_conv_w2, L1_conv_ff_w0, L1_conv_ff_b0, L1_conv_ff_w1, L1_conv_ff_b1, L1_conv_ln_g, L1_conv_ln_b, L2_conv_in_proj_w, L2_conv_conv_w, L2_conv_conv_b, L2_conv_x_proj_w, L2_conv_dt_proj_w, L2_conv_dt_proj_b, L2_conv_A_logs, L2_conv_Ds, L2_conv_norm_g, L2_conv_norm_b, L2_conv_out_proj_w, L3_conv_w1, L3_conv_dw, L3_conv_in_proj_w, L3_conv_conv1d_w, L3_conv_conv1d_b, L3_conv_x_proj_w, L3_conv_dt_proj_w, L3_conv_dt_proj_b, L3_conv_A_log, L3_conv_D_param, L3_conv_out_proj_w, L3_conv_gamma, L3_conv_beta, L3_conv_w2, L3_conv_wout):
    import jax
    import jax.numpy as jnp
    def _L0_conv_ref(x, w_qkv, w_out, b_out, g_ln, b_ln):
        import jax, jax.numpy as jnp
        import numpy as np
        HEADS = 4
        DIM_HEAD = 32
        EPS = 1e-05
        B, H, W, C = x.shape
        scale = DIM_HEAD ** (-0.5)
        n = H * W
        qkv = jnp.einsum('bhwc,cf->bhwf', x, w_qkv)
        q, k, v = jnp.split(qkv, 3, axis=-1)

        def to_heads(t):
            return t.reshape(B, n, HEADS, DIM_HEAD).transpose(0, 2, 3, 1)
        q, k, v = map(to_heads, (q, k, v))
        q = jax.nn.softmax(q, axis=-2) * scale
        k = jax.nn.softmax(k, axis=-1)
        context = jnp.einsum('bhdn,bhen->bhde', k, v)
        out = jnp.einsum('bhde,bhdn->bhen', context, q)
        out = out.transpose(0, 3, 1, 2).reshape(B, H, W, HEADS * DIM_HEAD)
        out = jnp.einsum('bhwc,cd->bhwd', out, w_out) + b_out
        mean = jnp.mean(out, axis=-1, keepdims=True)
        var = jnp.var(out, axis=-1, keepdims=True)
        out = (out - mean) / jnp.sqrt(var + EPS) * g_ln + b_ln
        return out

    def _L1_conv_ref(x, w1, w2, ff_w0, ff_b0, ff_w1, ff_b1, ln_g, ln_b):
        import jax, jax.numpy as jnp
        import numpy as np
        LN_EPS = 1e-05

        def _layer_norm(h, g, b):
            mu = jnp.mean(h, axis=-1, keepdims=True)
            var = jnp.mean(jnp.square(h - mu), axis=-1, keepdims=True)
            return (h - mu) * jax.lax.rsqrt(var + LN_EPS) * g + b

        def _forward_fourier(x, w1, w2):
            xt = jnp.transpose(x, (0, 3, 1, 2))
            B, I, M, N = xt.shape
            nm = w1.shape[2]
            cw1 = w1[..., 0] + 1j * w1[..., 1]
            cw2 = w2[..., 0] + 1j * w2[..., 1]
            O = cw1.shape[1]
            fty = jnp.fft.rfft(xt, axis=-1, norm='ortho')
            f1 = jnp.einsum('bixy,ioy->boxy', fty[..., :nm], cw1)
            pad_y = jnp.zeros((B, O, M, N // 2 + 1 - nm), dtype=f1.dtype)
            xy = jnp.fft.irfft(jnp.concatenate([f1, pad_y], axis=-1), n=N, axis=-1, norm='ortho')
            ftx = jnp.fft.rfft(xt, axis=-2, norm='ortho')
            f2 = jnp.einsum('bixy,iox->boxy', ftx[:, :, :nm, :], cw2)
            pad_x = jnp.zeros((B, O, M // 2 + 1 - nm, N), dtype=f2.dtype)
            xx = jnp.fft.irfft(jnp.concatenate([f2, pad_x], axis=-2), n=M, axis=-2, norm='ortho')
            return jnp.transpose(xx + xy, (0, 2, 3, 1))
        h = _forward_fourier(x, w1, w2)
        h1 = jax.nn.relu(jnp.einsum('bmni,ih->bmnh', h, ff_w0) + ff_b0)
        h2 = jnp.einsum('bmnh,ho->bmno', h1, ff_w1) + ff_b1
        return _layer_norm(h2, ln_g, ln_b)

    def _L2_conv_ref(x, in_proj_w, conv_w, conv_b, x_proj_w, dt_proj_w, dt_proj_b, A_logs, Ds, norm_g, norm_b, out_proj_w):
        import jax, jax.numpy as jnp
        import numpy as np
        from jax import lax
        B, H, W, C = (4, 48, 48, 128)
        D_INNER, D_STATE, DT_RANK, K = (256, 16, 8, 4)
        B, H, W, C = x.shape
        d = in_proj_w.shape[0] // 2
        K = x_proj_w.shape[0]
        N = A_logs.shape[1]
        R = x_proj_w.shape[1] - 2 * N
        L = H * W
        xz = jnp.einsum('bhwc,ec->bhwe', x, in_proj_w)
        xin, z = jnp.split(xz, 2, axis=-1)
        xc = jnp.transpose(xin, (0, 3, 1, 2))
        xc = lax.conv_general_dilated(xc, conv_w, (1, 1), [(1, 1), (1, 1)], feature_group_count=d, dimension_numbers=('NCHW', 'OIHW', 'NCHW'))
        xc = jax.nn.silu(xc + conv_b[None, :, None, None])
        x0 = xc.reshape(B, d, L)
        x1 = jnp.transpose(xc, (0, 1, 3, 2)).reshape(B, d, L)
        xs = jnp.stack([x0, x1, x0[..., ::-1], x1[..., ::-1]], axis=1)
        x_dbl = jnp.einsum('bkdl,kcd->bkcl', xs, x_proj_w)
        dts_r, Bs, Cs = (x_dbl[:, :, :R], x_dbl[:, :, R:R + N], x_dbl[:, :, R + N:])
        dts = jnp.einsum('bkrl,kdr->bkdl', dts_r, dt_proj_w)
        dt = jax.nn.softplus(dts + dt_proj_b[None, :, :, None])
        A = -jnp.exp(A_logs).reshape(K, d, N)
        dt_t = jnp.moveaxis(dt, -1, 0)
        u_t = jnp.moveaxis(xs, -1, 0)
        B_t = jnp.moveaxis(Bs, -1, 0)
        C_t = jnp.moveaxis(Cs, -1, 0)

        def step(h, inp):
            dt_l, u_l, B_l, C_l = inp
            dA = jnp.exp(dt_l[..., None] * A)
            h = h * dA + (dt_l * u_l)[..., None] * B_l[:, :, None, :]
            y = jnp.einsum('bkdn,bkn->bkd', h, C_l)
            return (h, y)
        h0 = jnp.zeros((B, K, d, N), x.dtype)
        _, ys = lax.scan(step, h0, (dt_t, u_t, B_t, C_t))
        ys = jnp.moveaxis(ys, 0, -1)
        ys = ys + Ds.reshape(1, K, d, 1) * xs
        y = ys[:, 0] + ys[:, 2][..., ::-1]
        y1 = ys[:, 1] + ys[:, 3][..., ::-1]
        y = y + jnp.transpose(y1.reshape(B, d, W, H), (0, 1, 3, 2)).reshape(B, d, L)
        y = jnp.transpose(y, (0, 2, 1))
        mu = jnp.mean(y, -1, keepdims=True)
        var = jnp.var(y, -1, keepdims=True)
        y = (y - mu) * lax.rsqrt(var + 1e-05) * norm_g + norm_b
        y = y.reshape(B, H, W, d) * jax.nn.silu(z)
        return jnp.einsum('bhwd,cd->bhwc', y, out_proj_w)

    def _L3_conv_ref(x, w1, dw, in_proj_w, conv1d_w, conv1d_b, x_proj_w, dt_proj_w, dt_proj_b, A_log, D_param, out_proj_w, gamma, beta, w2, wout):
        import jax, jax.numpy as jnp
        import numpy as np
        D_STATE = 8
        DT_RANK = 8

        def _grouped_1x1(x, w):
            B, H, W, _ = x.shape
            g, o, i = w.shape
            xg = x.reshape(B, H, W, g, i)
            return jnp.einsum('bhwgi,goi->bhwgo', xg, w).reshape(B, H, W, g * o)

        def _mamba(x_seq, in_proj_w, conv1d_w, conv1d_b, x_proj_w, dt_proj_w, dt_proj_b, A_log, D_param, out_proj_w):
            B, L, D = x_seq.shape
            N, R = (D_STATE, DT_RANK)
            xz = jnp.einsum('bld,ed->ble', x_seq, in_proj_w)
            u, z = (xz[..., :D], xz[..., D:])
            up = jnp.pad(u, ((0, 0), (2, 0), (0, 0)))
            u = up[:, 0:L] * conv1d_w[:, 0] + up[:, 1:L + 1] * conv1d_w[:, 1] + up[:, 2:L + 2] * conv1d_w[:, 2] + conv1d_b
            u = jax.nn.silu(u)
            x_dbl = jnp.einsum('bld,ed->ble', u, x_proj_w)
            dt = x_dbl[..., :R]
            Bm = x_dbl[..., R:R + N]
            Cm = x_dbl[..., R + N:]
            delta = jax.nn.softplus(jnp.einsum('blr,dr->bld', dt, dt_proj_w) + dt_proj_b)
            A = -jnp.exp(A_log)

            def step(h, inp):
                d_t, u_t, b_t, c_t = inp
                dA = jnp.exp(d_t[..., None] * A)
                h = dA * h + (d_t * u_t)[..., None] * b_t[:, None, :]
                y_t = jnp.einsum('bdn,bn->bd', h, c_t)
                return (h, y_t)
            h0 = jnp.zeros((B, D, N), dtype=x_seq.dtype)
            xs = (jnp.swapaxes(delta, 0, 1), jnp.swapaxes(u, 0, 1), jnp.swapaxes(Bm, 0, 1), jnp.swapaxes(Cm, 0, 1))
            _, ys = jax.lax.scan(step, h0, xs)
            y = jnp.swapaxes(ys, 0, 1) + u * D_param
            y = y * jax.nn.silu(z)
            return jnp.einsum('bld,ed->ble', y, out_proj_w)
        B, H, W, C = x.shape
        D = dw.shape[-1]
        x1 = _grouped_1x1(x, w1)
        x1 = jax.lax.conv_general_dilated(x1, dw, window_strides=(1, 1), padding='SAME', feature_group_count=D, dimension_numbers=('NHWC', 'HWIO', 'NHWC'))
        x1 = jax.nn.silu(x1)
        x1_seq = x1.reshape(B, H * W, D)
        x1_seq = _mamba(x1_seq, in_proj_w, conv1d_w, conv1d_b, x_proj_w, dt_proj_w, dt_proj_b, A_log, D_param, out_proj_w)
        x1 = x1_seq.reshape(B, H, W, D)
        mu = jnp.mean(x1, axis=-1, keepdims=True)
        var = jnp.mean(jnp.square(x1 - mu), axis=-1, keepdims=True)
        x1 = (x1 - mu) * jax.lax.rsqrt(var + 1e-05) * gamma + beta
        x2 = jax.nn.silu(_grouped_1x1(x, w2))
        x_fuse = x1 * x2
        return _grouped_1x1(x_fuse, wout)

    def _gn(v, G=32, eps=1e-5):
        B_, H_, W_, C_ = v.shape
        g = v.reshape(B_, H_, W_, G, C_ // G)
        m = jnp.mean(g, axis=(1, 2, 4), keepdims=True)
        s = jnp.var(g, axis=(1, 2, 4), keepdims=True)
        return ((g - m) / jnp.sqrt(s + eps)).reshape(v.shape)

    def _ln_c(v, eps=1e-6):
        m = jnp.mean(v, axis=-1, keepdims=True)
        s = jnp.var(v, axis=-1, keepdims=True)
        return (v - m) / jnp.sqrt(s + eps)

    def _ln_t(v, eps=1e-5):
        m = jnp.mean(v, axis=-1, keepdims=True)
        s = jnp.var(v, axis=-1, keepdims=True)
        return (v - m) / jnp.sqrt(s + eps)

    def _to_tokens(v):
        B_, H_, W_, C_ = v.shape
        return v.reshape(B_, H_ * W_, C_)
    def _from_tokens(t, like):
        return t.reshape(like.shape)

    x = x + _L0_conv_ref(_gn(x), L0_conv_w_qkv, L0_conv_w_out, L0_conv_b_out, L0_conv_g_ln, L0_conv_b_ln)
    x = x + _L1_conv_ref(_gn(x), L1_conv_w1, L1_conv_w2, L1_conv_ff_w0, L1_conv_ff_b0, L1_conv_ff_w1, L1_conv_ff_b1, L1_conv_ln_g, L1_conv_ln_b)
    x = x + _L2_conv_ref(_gn(x), L2_conv_in_proj_w, L2_conv_conv_w, L2_conv_conv_b, L2_conv_x_proj_w, L2_conv_dt_proj_w, L2_conv_dt_proj_b, L2_conv_A_logs, L2_conv_Ds, L2_conv_norm_g, L2_conv_norm_b, L2_conv_out_proj_w)
    x = x + _L3_conv_ref(_gn(x), L3_conv_w1, L3_conv_dw, L3_conv_in_proj_w, L3_conv_conv1d_w, L3_conv_conv1d_b, L3_conv_x_proj_w, L3_conv_dt_proj_w, L3_conv_dt_proj_b, L3_conv_A_log, L3_conv_D_param, L3_conv_out_proj_w, L3_conv_gamma, L3_conv_beta, L3_conv_w2, L3_conv_wout)
    return x


_drawn_inputs = setup_inputs


def setup_inputs(seed=0):
    import zlib

    import numpy as np

    out = dict(_drawn_inputs(seed))
    spreads = {'L0_conv_b_out': (0.0, 0.1),
     'L0_conv_g_ln': (1.0, 0.2),
     'L0_conv_b_ln': (0.0, 0.1),
     'L1_conv_ff_b0': (0.0, 0.1),
     'L1_conv_ff_b1': (0.0, 0.1),
     'L1_conv_ln_g': (1.0, 0.2),
     'L1_conv_ln_b': (0.0, 0.1),
     'L2_conv_conv_b': (0.0, 0.1),
     'L2_conv_Ds': (1.0, 0.6),
     'L2_conv_norm_g': (1.0, 0.2),
     'L2_conv_norm_b': (0.0, 0.277),
     'L3_conv_D_param': (1.0, 0.6),
     'L3_conv_gamma': (1.0, 0.6),
     'L3_conv_beta': (0.0, 0.792)}
    factors = {'L0_conv_w_qkv': 7.264,
     'L0_conv_w_out': 7.257,
     'L2_conv_dt_proj_w': 4.728,
     'L2_conv_dt_proj_b': 5.375,
     'L3_conv_w1': 4.134,
     'L3_conv_dw': 4.445,
     'L3_conv_in_proj_w': 4.255,
     'L3_conv_conv1d_w': 8.0,
     'L3_conv_conv1d_b': 3.678,
     'L3_conv_x_proj_w': 8.0,
     'L3_conv_dt_proj_w': 8.0,
     'L3_conv_dt_proj_b': 8.0,
     'L3_conv_A_log': 8.0,
     'L3_conv_out_proj_w': 3.74,
     'L3_conv_w2': 3.533,
     'L3_conv_wout': 3.105}
    for name, (base, spread) in spreads.items():
        noise = np.random.default_rng([zlib.crc32(name.encode()), seed]).standard_normal(out[name].shape)
        drawn = base * np.exp(spread * noise) if base else spread * noise
        out[name] = jnp.asarray(drawn.astype(out[name].dtype))
    for name, factor in factors.items():
        out[name] = (out[name] * factor).astype(out[name].dtype)
    return out
```

```python
import numpy as np
import concourse.bass as bass
from concourse import mybir
from contextlib import ExitStack

LAYERS = 4
P = 128
HW = 64
L = HW * HW
NT = 512
NCH = L // NT
ROWS = NT // HW
PW = HW + 2
MODES = 16
HEADS, DH = 4, 32
KDIR = 4
SN = 16
SN3 = 8
RANK = 8
GROUPS = 32


def shape_constants():
    f = np.float32
    eye = np.eye(P, dtype=f)
    cen = eye - f(1.0 / P)
    ones = np.full((P, P), 1.0 / P, f)
    grp = np.kron(np.eye(GROUPS), np.full((P // GROUPS,) * 2, GROUPS / P)).astype(f)
    head = np.kron(np.eye(HEADS), np.ones((DH, DH))).astype(f)
    y, w = np.arange(MODES), np.arange(HW)
    ang = 2 * np.pi * np.outer(w, y) / HW
    fwd = np.stack([np.cos(ang), -np.sin(ang)], 2) / np.sqrt(HW)
    fw = np.zeros((2, HW, MODES, 2, 2)); fh = np.zeros((HW, 2, MODES, 2, 2))
    for r in range(2):
        fw[r, :, :, :, r] = fwd
        fh[:, r, :, :, r] = fwd
    c = np.where(y == 0, 1.0, 2.0)[:, None] / np.sqrt(HW)
    inv = np.stack([c * np.cos(ang.T), -c * np.sin(ang.T)], 1)
    fi = np.zeros((4, MODES, 2, 4, HW))
    for m in range(4):
        fi[m, :, :, m, :] = inv
    onehot = np.zeros((P, 32)); onehot[np.arange(96), np.arange(96) % 32] = 1
    m1 = np.zeros((P, 1)); m1[32:96] = -1
    m2 = np.zeros((P, 1)); m2[64:96] = -1
    return np.concatenate([eye, cen, ones, grp, head, fw.reshape(P, 64), fh.reshape(P, 64),
                           fi.reshape(P, 256), onehot, m1, m2], 1).astype(f)


CONST_COLS = {}
_at = 0
for _n, _w in (("eye", P), ("cen", P), ("ones", P), ("grp", P), ("head", P), ("fw", 64), ("fh", 64),
               ("fi", 256), ("onehot", 32), ("m1", 1), ("m2", 1)):
    CONST_COLS[_n] = (_at, _at + _w)
    _at += _w
NCONST = _at


def program(nc, x_in, consts, d, out):
    fp32, bf16 = mybir.dt.float32, mybir.dt.bfloat16
    ALU, ACT, AXX = mybir.AluOpType, mybir.ActivationFunctionType, mybir.AxisListType.X
    MUL, ADD, SUB, MAX = ALU.mult, ALU.add, ALU.subtract, ALU.max
    B = x_in.shape[0]
    ctx = ExitStack()
    with ctx:
        def sb(name, cols, dt=fp32):
            return ctx.enter_context(nc.sbuf_tensor(name, [P, cols], dt))

        persistent = []

        def sem(name):
            s = ctx.enter_context(nc.semaphore(name))
            return s

        def sample_sem(name):
            s = sem(name)
            persistent.append(s)
            return s

        X = sb("X", L)
        XN = sb("XN", PW * PW)
        BIG1 = sb("BIG1", 2 * L + 8)
        BIG2 = sb("BIG2", 2 * L)
        WORK = sb("WORK", 14848)
        CST = sb("CST", NCONST)
        WK = sb("WK", P); WQV = sb("WQV", 2 * P); WO0 = sb("WO0", P)
        FW0 = sb("FW0", 4 * P); FW1 = sb("FW1", 4 * P)
        WZ2 = sb("WZ2", 2 * P); TAP2 = sb("TAP2", 9 * 2 * P); WO2 = sb("WO2", 2 * P)
        XP2 = sb("XP2", KDIR * 2 * 104); DTW2 = sb("DTW2", KDIR * 2 * P)
        DTB2 = sb("DTB2", KDIR * 2); AN2 = sb("AN2", KDIR * 2 * SN)
        BD1 = sb("BD1", P); TAP3 = sb("TAP3", 9 * P); WU3 = sb("WU3", P); TAPU3 = sb("TAPU3", 3 * P)
        WZ3 = sb("WZ3", P); XP3 = sb("XP3", 104); DTW3 = sb("DTW3", P); DTB3 = sb("DTB3", 1)
        AN3 = sb("AN3", SN3); WO3 = sb("WO3", P); W23 = sb("W23", P); WOUT3 = sb("WOUT3", P)
        SEL = sb("SEL", 32 * P, bf16)
        VEC = sb("VEC", 64)
        SM = sb("SM", 64)
        GST = sb("GST", NCH * 6)
        HST2 = sb("HST2", 2 * SN); HST3 = sb("HST3", SN3)

        names = ["b_out", "b_out_c", "g0", "b0", "ffb1", "ffb1_c", "g1", "b1", "ffb0_0", "ffb0_1", "ffb0_2",
                 "ffb0_3", "cb0", "cb1", "ng0", "ng1", "nb0", "nb1", "D0", "D1", "D2", "D3", "D4", "D5", "D6",
                 "D7", "Dt0", "Dt1", "cb3", "Dp3", "gam3", "bet3", "eps", "one", "mhalf", "edge"]
        vec = {n: VEC[:, i:i + 1] for i, n in enumerate(names)}
        vcol = {n: i for i, n in enumerate(names)}
        cst = {n: CST[:, a:b] for n, (a, b) in CONST_COLS.items()}
        EYE = cst["eye"]

        PS = ctx.enter_context(nc.psum_tensor("PS", [P, 8, NT], fp32))

        def bank(i):
            return PS[:, i, :]

        XNF = XN[:, 0:L]
        XN3 = XN[:, :].rearrange("p (h w) -> p h w", w=PW)

        def xn_tap(j, t):
            r, c = ROWS * j + t // 3, t % 3
            return XN3[:, r:r + ROWS, c:c + HW]

        def xn_mid(j):
            return xn_tap(j, 4)

        def ch(j, w=NT):
            return slice(j * w, (j + 1) * w)

        KC = BIG1[:, 0:L]
        KT = BIG1[:, L:2 * L]
        VT = WORK[:, 0:L]
        QT = WORK[:, L:2 * L]
        QC = WORK[:, 2 * L:3 * L]
        L0S = sb("L0S", 4 * P + 16)
        CT, M2S, QS, QMX = (L0S[:, P * i:P * i + P] for i in range(4))
        KMX = L0S[:, 4 * P:4 * P + 12]
        T0 = 3 * L
        SQ = [WORK[:, T0 + NT * i:T0 + NT * (i + 1)] for i in range(2)]
        RS = [WORK[:, T0 + NT * i:T0 + NT * (i + 1)] for i in (2, 3)]
        LV = WORK[:, T0 + 4 * NT:T0 + 5 * NT]
        SPEC = BIG2[:, :].rearrange("p (x y r o) -> p x y r o", x=2, y=MODES, r=2)
        HF = BIG1[:, 0:L]
        XT = [WORK[:, NT * i:NT * (i + 1)] for i in range(2)]
        S1 = [a.rearrange("p (y b m) -> p y b m", y=MODES, b=3)
              for a in (BIG1[:, L:L + 3 * 1024], WORK[:, 1024:4096])]
        FS = [WORK[:, L + 2048 * i:L + 2048 * (i + 1)] for i in range(2)]
        FT = [WORK[:, 2 * L + 2048 * i:2 * L + 2048 * (i + 1)] for i in range(2)]
        H1 = [WORK[:, 2048 * i:2048 * (i + 1)] for i in range(2)]
        TB = [sb(f"TB{i}", NT, bf16) for i in range(2)]

        class Scan:

            def __init__(s, tag, halves, states, dirs, at, u0, y0, xp, dtw, dtb, an, hst, d0):
                s.tag, s.halves, s.states, s.dirs = tag, halves, states, dirs
                (s.p_xp, s.p_c1, s.p_r1, s.p_c2, s.p_r2, s.p_c3, s.p_dt, s.p_sp, s.p_cb, s.p_du) = at
                w = halves * NT
                at_col = [0]

                def take(n):
                    at_col[0] += n
                    return WORK[:, at_col[0] - n:at_col[0]]
                s.A = [take(w) for _ in range(2)]
                s.Bq = [take(w) for _ in range(4)]
                s.DT = [take(w) for _ in range(2)]
                s.DU = [take(w) for _ in range(2)]
                s.Bs = [take(NT) for _ in range(2)]
                s.R = take(NT)
                s.TA, s.E, s.LE, s.RL, s.MK = (take(NT) for _ in range(5))
                s.u0, s.y0 = u0, y0
                s.XP, s.DTW, s.DTB, s.AN, s.HST, s.D = xp, dtw, dtb, an, hst, d0
                s.rows_ready = sample_sem(tag + "_rows_ready")
                s.split_cast = sample_sem(tag + "_split_cast")
                s.split_rest = sample_sem(tag + "_split_rest")
                s.dt_raw = sample_sem(tag + "_dt_raw")
                s.softplus = sample_sem(tag + "_softplus")
                s.dt_steps = sample_sem(tag + "_dt_steps")
                s.du_ready = sample_sem(tag + "_du_ready")
                s.b_bcast = sample_sem(tag + "_b_bcast")
                s.b_copied = sample_sem(tag + "_b_copied")
                s.c_bcast = sample_sem(tag + "_c_bcast")
                s.decay = sample_sem(tag + "_decay")
                s.drive = sample_sem(tag + "_drive")
                s.scanned = sample_sem(tag + "_scanned")
                s.carried = sample_sem(tag + "_carried")
                s.weighed = sample_sem(tag + "_weighed")
                s.summed = sample_sem(tag + "_summed")
                s.y_taken = sample_sem(tag + "_y_taken")

            def cols(s, big, start, k, pos):
                v = big[:, start:start + s.halves * L]
                if k % 2 == 0:
                    return v.rearrange("p (d l) -> p d l", l=L)[:, :, bass.ds(pos * NT, NT)]
                return v.rearrange("p (d h w) -> p d w h", h=HW, w=HW)[:, :, bass.ds(pos * ROWS, ROWS), :]

            def like(s, ap, k):
                if k % 2 == 0:
                    return ap.rearrange("p (d l) -> p d l", l=NT)
                return ap.rearrange("p (d w h) -> p d w h", w=ROWS, h=HW)

            def position(s, k, c):
                return c if k < 2 else c * -1 + (NCH - 1)

            def chunks(s, e, body):
                def pair(k, c, before, after):
                    body(k, c, 0, before, (k, c + 1))
                    body(k, c + 1, 1, (k, c), after)
                for k in range(s.dirs):
                    pair(k, 0, (k - 1, NCH - 1) if k else None, (k, 2))
                    with e.Fori(1, NCH // 2 - 1) as i:
                        pair(k, 2 * i, (k, 2 * i - 1), (k, 2 * i + 2))
                    pair(k, NCH - 2, (k, NCH - 3), (k + 1, 0) if k + 1 < s.dirs else None)

        S2 = Scan("s2", 2, SN, KDIR, (0, 4, 4, 7, 7, 10, 4, (8, 11), (8, 11), 15), 0, 0, XP2, DTW2, DTB2, AN2, HST2, None)
        S3 = Scan("s3", 1, SN3, 1, (0, 2, 2, 4, 4, 6, 2, (4,), (5,), 7), L + 4, 0, XP3, DTW3, DTB3, AN3, HST3, None)

        def after(e, s, per_chunk, k, c, off):
            v = c * per_chunk + (k * NCH * per_chunk + off)
            if isinstance(v, int) and v <= 0:
                return
            e.wait_ge(s, v)

        Z2 = BIG1[:, :2 * L].rearrange("p (d l) -> p d l", l=L)
        Y2 = BIG2[:, :].rearrange("p (d l) -> p d l", l=L)
        Q2 = [WORK[:, 1024 * i:1024 * (i + 1)].rearrange("p (d l) -> p d l", l=NT) for i in range(2)]
        R2 = [WORK[:, 2048 + NT * i:2048 + NT * (i + 1)] for i in range(2)]
        LV2 = WORK[:, 3072:3584]
        X1 = BIG1[:, 0:L + 2]
        X2G = BIG1[:, 0:L]
        U3 = BIG1[:, L + 4:2 * L + 4]
        Y3 = BIG2[:, 0:L]
        Z3 = BIG2[:, L:2 * L]

        weights_in = sem("weights_in"); zeroed = sem("zeroed"); vec_setup = sem("vec_setup")
        act_setup = sem("act_setup"); pe_setup = sem("pe_setup"); vec_ready = sem("vec_ready")
        sample_done = sem("sample_done"); next_sample = sem("next_sample")
        x_loaded = sample_sem("x_loaded"); spec_loaded = sample_sem("spec_loaded"); x_stored = sample_sem("x_stored")
        act_chain = sample_sem("act_chain"); dve_chain = sample_sem("dve_chain")
        gn_stats = sample_sem("gn_stats"); gn_mean = sample_sem("gn_mean"); gn_var = sample_sem("gn_var")
        gn_gvar = sample_sem("gn_gvar"); gn_rstd = sample_sem("gn_rstd"); xn_ready = sample_sem("xn_ready")
        frame_zero = sample_sem("frame_zero")
        k_proj = sample_sem("k_proj"); k_copied = sample_sem("k_copied"); k_max = sample_sem("k_max")
        k_shift = sample_sem("k_shift"); k_exp = sample_sem("k_exp"); qv_proj = sample_sem("qv_proj")
        v_copied = sample_sem("v_copied"); q_shifted = sample_sem("q_shifted"); q_exp = sample_sem("q_exp")
        q_norm = sample_sem("q_norm"); kT_made = sample_sem("kT_made"); kT_copied = sample_sem("kT_copied")
        qT_made = sample_sem("qT_made"); qT_copied = sample_sem("qT_copied"); ctx_made = sample_sem("ctx_made")
        ctx_masked = sample_sem("ctx_masked"); m2_made = sample_sem("m2_made"); m2_ready = sample_sem("m2_ready")
        t_proj = sample_sem("t_proj"); t_sq = sample_sem("t_sq"); t_var = sample_sem("t_var")
        t_rstd = sample_sem("t_rstd"); t_norm = sample_sem("t_norm"); x_added = sample_sem("x_added")
        f_trans = sample_sem("f_trans"); f_transc = sample_sem("f_transc"); f_spec = sample_sem("f_spec")
        f_specn = sample_sem("f_specn"); f_specp = sample_sem("f_specp"); f_mix = sample_sem("f_mix")
        f_mixc = sample_sem("f_mixc"); f_mixT = sample_sem("f_mixT"); f_mixTc = sample_sem("f_mixTc")
        f_inv = sample_sem("f_inv"); f_sum = sample_sem("f_sum"); h_proj = sample_sem("h_proj")
        h_reluA = sample_sem("h_reluA"); h_reluV = sample_sem("h_reluV")
        conv_done = sample_sem("conv_done"); conv_act = sample_sem("conv_act")
        z_proj = sample_sem("z_proj"); z_act = sample_sem("z_act")
        y_mean = sample_sem("y_mean"); y_cent = sample_sem("y_cent"); y_sq = sample_sem("y_sq")
        y_var = sample_sem("y_var"); y_rstd = sample_sem("y_rstd"); y_norm = sample_sem("y_norm")
        y_gated = sample_sem("y_gated"); y_out = sample_sem("y_out"); y_added = sample_sem("y_added")
        c3_done = sample_sem("c3_done"); c3_act = sample_sem("c3_act"); u3_proj = sample_sem("u3_proj")
        u3_act = sample_sem("u3_act"); g3_gated = sample_sem("g3_gated"); g3_fused = sample_sem("g3_fused")
        g3_out = sample_sem("g3_out"); pad3 = sample_sem("pad3"); z3_proj = sample_sem("z3_proj"); z3_act = sample_sem("z3_act")

        block = ctx.enter_context(nc.Block())

        w3 = lambda ap, **k: ap.rearrange("p (a b) -> p a b", **k)
        XP2v = XP2[:, :].rearrange("p (k d c) -> p k d c", k=KDIR, d=2)
        LOADS = [(CST[:, :], consts), (VEC[:, 0:len(names)], d["vecs"]), (WK[:, :], d["wk"]), (WQV[:, :], d["wqv"]),
                 (WO0[:, :], d["wo0"]), (FW0[:, :], d["ffw0"]), (w3(FW1[:, :], a=4), d["ffw1"]),
                 (BIG1[:, 0:2 * P], d["inpx"]), (WZ2[:, :], d["inpz"]),
                 (TAP2[:, :], d["cw2"].partition_broadcast(P)), (WO2[:, :], d["wo2"]),
                 (DTW2[96:96 + RANK, :], d["dtw2"]), (DTB2[:, :], d["dtb2"]), (AN2[:, :], d["al2"]),
                 (TAP3[:, :], d["dw3"].partition_broadcast(P)), (WU3[:, :], d["inpu3"]), (WZ3[:, :], d["inpz3"]),
                 (TAPU3[:, :], d["cw3"].partition_broadcast(P)), (DTW3[96:96 + RANK, :], d["dtw3"]),
                 (DTB3[:, :], d["dtb3"]), (AN3[:, :], d["al3"]), (WO3[:, :], d["wo3"]), (XP3[:, 96:104], d["xdt3"])]
        LOADS += [(XP2v[:, :, :, 96:104], d["xdt2"])]
        LOADS += [(XP2v[:, :, :, 32 * r:32 * r + 32], d["xbc2"]) for r in range(3)]
        BLOCKS = [(t[32 * g:32 * g + 32, 32 * g:32 * g + 32], d[n][g]) for t, n in
                  ((BD1, "w1"), (W23, "w2"), (WOUT3, "wout")) for g in range(4)]
        BLOCKS += [(XP3[:, 32 * r:32 * r + 2 * SN3], d["xbc3"]) for r in range(3)]
        NLOADS = 16 * (len(LOADS) + len(BLOCKS))

        @block.sync
        def _(e):
            for dst, src in LOADS:
                e.dma_start(dst, src).then_inc(weights_in, 16)
            e.wait_ge(zeroed, 4)
            for dst, src in BLOCKS:
                e.dma_start(dst, src).then_inc(weights_in, 16)
            e.wait_ge(pe_setup, 1)
            with e.Fori(0, B) as b:
                e.dma_start(X[:, :], x_in[bass.ds(b, 1), :, :].rearrange("o p l -> (o p) l")).then_inc(x_loaded, 16)
                e.dma_start(BIG2[:, 0:L], d["spec1"]).then_inc(spec_loaded, 16)
                e.dma_start(BIG2[:, L:2 * L], d["spec2"]).then_inc(spec_loaded, 16)
                e.wait_ge(x_added, NCH * LAYERS)
                e.dma_start(out[bass.ds(b, 1), :, :].rearrange("o p l -> (o p) l"), X[:, :]).then_inc(x_stored, 16)
                e.wait_ge(x_stored, 16)
                e.wait_ge(sample_done, 4)
                for s in persistent + [sample_done]:
                    e.sem_clear(s)
                e.sem_inc(next_sample, 1)

        def meet(e, b):
            e.sem_inc(sample_done, 1)
            e.wait_ge(next_sample, b + 1)

        @block.gpsimd
        def _(e):
            for t in (BD1, W23, WOUT3):
                nc.gpsimd.memset(t[:, :], 0.0).then_inc(zeroed, 1)
            nc.gpsimd.memset(XP3[:, 0:96], 0.0).then_inc(zeroed, 1)

            def scan(S):
                w, N = S.halves, S.states

                def make_du(k, c, par):
                    after(e, S.dt_steps, 4 * w, k, c, 4 * w)
                    after(e, S.drive, N, k, c, -N)
                    pos = S.position(k, c)
                    nc.gpsimd.tensor_tensor(S.like(S.DU[par], k), S.like(S.DT[par], k), S.cols(BIG1, S.u0, k, pos),
                                            MUL).then_inc(S.du_ready, 1)

                def body(k, c, par, prv, nxt):
                    for n in range(N):
                        if n == 0:
                            after(e, S.du_ready, 1, k, c, 1)
                        after(e, S.b_copied, N, k, c, n + 1)
                        after(e, S.summed, N, k, c, n - 3)
                        q = S.Bq[n % 4].rearrange("p (d l) -> p d l", l=NT)
                        u = S.DU[par].rearrange("p (d l) -> p d l", l=NT)
                        nc.gpsimd.tensor_tensor(q, u, S.Bs[n % 2].unsqueeze(1).to_broadcast([P, w, NT]),
                                                MUL).then_inc(S.drive, 1)
                        if nxt and n == S.p_du:
                            make_du(*nxt, 1 - par)

                make_du(0, 0, 0)
                S.chunks(e, body)

            with e.Fori(0, B) as b:
                if LAYERS > 2:
                    e.wait_ge(gn_stats, 3)
                    nc.gpsimd.memset(XN3[:, 0, :], 0.0).then_inc(frame_zero, 1)
                    nc.gpsimd.memset(XN3[:, PW - 1, :], 0.0).then_inc(frame_zero, 1)
                    edge = XN[:, PW - 1:PW - 1 + (PW - 1) * PW].rearrange("p (h w) -> p h w", w=PW)[:, :, 0:2]
                    e.wait_ge(frame_zero, 2)
                    nc.gpsimd.memset(edge, 0.0).then_inc(frame_zero, 1)
                    scan(S2)
                    for j in range(NCH):
                        e.wait_ge(y_norm, j + 1)
                        e.wait_ge(z_act, 2 * NCH)
                        nc.gpsimd.tensor_tensor(Y2[:, :, ch(j)], Y2[:, :, ch(j)], Z2[:, :, ch(j)], MUL).then_inc(y_gated, 1)
                if LAYERS > 3:
                    e.wait_ge(y_gated, NCH)
                    e.wait_ge(y_out, NCH)
                    nc.gpsimd.memset(X1[:, 0:2], 0.0).then_inc(pad3, 1)
                    scan(S3)
                    for j in range(NCH):
                        e.wait_ge(S3.y_taken, j + 1)
                        e.wait_ge(z3_act, NCH)
                        nc.gpsimd.tensor_tensor(Y3[:, ch(j)], Y3[:, ch(j)], Z3[:, ch(j)], MUL).then_inc(g3_gated, 1)
                    e.wait_ge(g3_gated, NCH)
                meet(e, b)

        @block.tensor
        def _(e):
            def mm(o, w, r, start=True, stop=True):
                return nc.tensor.matmul(o, w, r, start=start, stop=stop)

            def group_norm(layer):
                e.wait_ge(gn_stats, layer + 1)
                mm(bank(7)[:, 0:1], cst["grp"], SM[:, 0:1]).then_inc(gn_mean, 1)
                e.wait_ge(gn_var, layer + 1)
                mm(bank(7)[:, 1:2], cst["grp"], SM[:, 4:5]).then_inc(gn_gvar, 1)
                e.wait_ge(xn_ready, 2 * layer + 2)

            def tail(layer, project):
                base = NCH * min(layer, 2)

                def variance(j):
                    e.wait_ge(t_sq, base + j + 1)
                    if base + j >= 2:
                        e.wait_ge(t_rstd, base + j - 1)
                    mm(bank(2 + j % 2), cst["ones"], SQ[j % 2]).then_inc(t_var, 1)

                for j in range(NCH):
                    if base + j >= 2:
                        e.wait_ge(t_norm, base + j - 1)
                    project(j).then_inc(t_proj, 1)
                    if j:
                        variance(j - 1)
                variance(NCH - 1)

            def block0():
                for j in range(NCH):
                    if j >= 2:
                        e.wait_ge(k_copied, j - 1)
                    mm(bank(j % 2), WK[:, :], XNF[:, ch(j)]).then_inc(k_proj, 1)
                for g in range(2 * NCH):
                    if g >= 4:
                        e.wait_ge(v_copied, g - 3)
                        e.wait_ge(q_shifted, g - 3)
                    for i in range(2):
                        r = mm(bank(2 + g % 4)[:, 256 * i:256 * (i + 1)], XNF[:, ch(2 * g + i, P)], WQV[:, :])
                    r.then_inc(qv_proj, 1)
                e.wait_ge(k_exp, 1)
                e.wait_ge(v_copied, 2 * NCH)

                def context(g):
                    e.wait_ge(kT_copied, g + 1)
                    for t in range(4 * g, 4 * g + 4):
                        r = mm(bank(6)[:, 0:P], VT[:, ch(t, P)], KT[:, ch(t, P)], t == 0, t == L // P - 1)
                    return r
                for g in range(NCH):
                    if g >= 2:
                        e.wait_ge(kT_copied, g - 1)
                    for i in range(4):
                        r = nc.tensor.transpose(bank(g % 2)[:, ch(i, P)], KC[:, ch(4 * g + i, P)], EYE)
                    r.then_inc(kT_made, 1)
                    if g:
                        context(g - 1)
                context(NCH - 1).then_inc(ctx_made, 1)
                for g in range(NCH):
                    e.wait_ge(q_norm, g // 2 + 1)
                    if g >= 2:
                        e.wait_ge(qT_copied, g - 1)
                    for i in range(4):
                        r = nc.tensor.transpose(bank(2 + g % 2)[:, ch(i, P)], QT[:, ch(4 * g + i, P)], EYE)
                    r.then_inc(qT_made, 1)
                e.wait_ge(ctx_masked, 1)
                mm(bank(6)[:, P:2 * P], CT, WO0[:, :]).then_inc(m2_made, 1)
                e.wait_ge(m2_ready, 1)
                e.wait_ge(qT_copied, NCH)
                tail(0, lambda j: mm(bank(j % 2), M2S, QC[:, ch(j)]))

            def block1():
                e.wait_ge(spec_loaded, 32)
                for x in range(2):
                    fwd = cst["fw" if x == 0 else "fh"]

                    def spectrum(g):
                        c = NCH * x + g
                        e.wait_ge(f_transc, c + 1)
                        if c // 2 >= 2 and g % 2 == 0:
                            e.wait_ge(f_specn, c // 2 - 1)
                            e.wait_ge(f_specp, 2 * (c // 2 - 1))
                        for i in range(4):
                            r = mm(bank(2 + (g // 2) % 2)[:, 256 * (g % 2) + 64 * i:256 * (g % 2) + 64 * (i + 1)],
                                   XT[g % 2][:, ch(i, P)], fwd)
                        if g % 2:
                            r.then_inc(f_spec, 1)

                    for g in range(NCH):
                        c = NCH * x + g
                        if c >= 2:
                            e.wait_ge(f_transc, c - 1)
                        for i in range(4):
                            t = 4 * g + i
                            tile = XNF[:, ch(t, P)] if x == 0 else XNF[:, t:L:HW // 2]
                            r = nc.tensor.transpose(bank(g % 2)[:, ch(i, P)], tile, EYE)
                        r.then_inc(f_trans, 1)
                        if g:
                            spectrum(g - 1)
                    spectrum(NCH - 1)
                for x in range(2):
                    for q in range(4):
                        c = 4 * x + q
                        e.wait_ge(f_specn, 4 * x + 4)
                        e.wait_ge(f_specp, 2 * (4 * x + 4))
                        if c >= 2:
                            e.wait_ge(f_mixc, c - 1)
                        for i in range(4):
                            y = 4 * q + i
                            o = bank(4 + q % 2)[:, ch(i, P)]
                            mm(o, SPEC[:, x, y, 0, :], S1[x][:, y, 1:3, :].rearrange("p b m -> p (b m)"), True, False)
                            r = mm(o, SPEC[:, x, y, 1, :], S1[x][:, y, 0:2, :].rearrange("p b m -> p (b m)"), False, True)
                        r.then_inc(f_mix, 1)
                for x in range(2):
                    for q in range(4):
                        c = 4 * x + q
                        e.wait_ge(f_mixc, 4 * x + 4)
                        if c >= 2:
                            e.wait_ge(f_mixTc, c - 1)
                        for i in range(4):
                            r = nc.tensor.transpose(bank(q % 2)[:, ch(i, P)], FS[x][:, ch(4 * q + i, P)], EYE)
                        r.then_inc(f_mixT, 1)
                for x in range(2):
                    for j in range(NCH):
                        c = NCH * x + j
                        e.wait_ge(f_mixTc, 4 * x + j // 2 + 1)
                        if c >= 2:
                            e.wait_ge(f_sum, c - 1)
                        for i in range(2):
                            r = mm(bank(2 + j % 2)[:, 256 * i:256 * (i + 1)], FT[x][:, ch(2 * j + i, P)], cst["fi"])
                        r.then_inc(f_inv, 1)
                e.wait_ge(f_sum, 2 * NCH)

                def hidden(j):
                    for f in range(4):
                        if j:
                            e.wait_ge((h_reluA, h_reluV)[f // 2], 2 * (j - 1) + f % 2 + 1)
                        mm(bank(4 + f), FW0[:, ch(f, P)], HF[:, ch(j)]).then_inc(h_proj, 1)

                def project(j):
                    if j == 0:
                        hidden(0)
                    if j + 1 < NCH:
                        hidden(j + 1)
                    e.wait_ge(h_reluA, 2 * j + 2)
                    e.wait_ge(h_reluV, 2 * j + 2)
                    for f in range(4):
                        r = mm(bank(j % 2), FW1[:, ch(f, P)], H1[j % 2][:, ch(f)], f == 0, f == 3)
                    return r
                tail(1, project)

            def scan(S):
                w, N = S.halves, S.states

                def rows(k, c, par):
                    after(e, S.split_rest, 2, k, c, 0)
                    after(e, S.softplus, 6 * w, k, c, 0)
                    pos = S.position(k, c)
                    src = S.cols(BIG1, S.u0, k, pos)
                    for h in range(w):
                        wt = S.XP[:, 104 * (w * k + h):104 * (w * k + h + 1)]
                        r = mm(S.like(bank(6), k)[0:104, 0] if k % 2 else bank(6)[0:104, :], wt, src[:, h], h == 0, h == w - 1)
                    r.then_inc(S.rows_ready, 1)

                def steps(k, c, h):
                    after(e, S.split_cast, 4, k, c, 2)
                    if h == 0:
                        after(e, S.softplus, 6 * w, k, c, 0)
                    else:
                        after(e, S.split_rest, 2, k, c, 1)
                    mm(bank(7 - h), S.DTW[96:96 + RANK, P * (w * k + h):P * (w * k + h + 1)], S.R[96:96 + RANK, :])\
                        .then_inc(S.dt_raw, 1)

                def bcast_b(k, c, par, n):
                    after(e, S.split_cast, 4, k, c, 4)
                    after(e, S.b_copied, N, k, c, n - 1)
                    mm(bank(4 + n % 2), SEL[0:96, ch(n, P)], TB[par][0:96, :]).then_inc(S.b_bcast, 1)

                def bcast_c(k, c, par, n):
                    after(e, S.split_cast, 4, k, c, 4)
                    after(e, S.weighed, N, k, c, n - 1)
                    mm(bank(2 + n % 2), SEL[0:96, ch(N + n, P)], TB[par][0:96, :]).then_inc(S.c_bcast, 1)

                def body(k, c, par, prv, nxt):
                    for n in range(N):
                        for f, ahead in ((bcast_b, 4), (bcast_c, 2)):
                            if n + ahead < N:
                                f(k, c, par, n + ahead)
                            elif nxt:
                                f(*nxt, 1 - par, n + ahead - N)
                        after(e, S.weighed, N, k, c, n + 1)
                        if n == 0:
                            after(e, S.y_taken, 1, k, c, 0)
                        for h in range(w):
                            r = mm(bank(h), EYE, S.Bq[n % 4][:, ch(h)], n == 0, n == N - 1)
                        r.then_inc(S.summed, 1)
                        if nxt and n == S.p_xp:
                            rows(*nxt, 1 - par)
                        if nxt and n == S.p_dt:
                            for h in range(w):
                                steps(*nxt, h)

                rows(0, 0, 0)
                for h in range(w):
                    steps(0, 0, h)
                bcast_b(0, 0, 0, 0)
                bcast_b(0, 0, 0, 1)
                bcast_c(0, 0, 0, 0)
                bcast_c(0, 0, 0, 1)
                bcast_b(0, 0, 0, 2)
                bcast_b(0, 0, 0, 3)
                S.chunks(e, body)

            def block2():
                e.wait_ge(frame_zero, 3)
                for j in range(NCH):
                    for h in range(2):
                        c = 2 * j + h
                        if c >= 4:
                            e.wait_ge(conv_act, c - 3)
                        for t in range(9):
                            r = mm(bank(c % 4), TAP2[:, 256 * t + P * h:256 * t + P * (h + 1)], xn_tap(j, t), t == 0, t == 8)
                        r.then_inc(conv_done, 1)
                e.wait_ge(conv_act, 2 * NCH)
                scan(S2)
                e.wait_ge(S2.y_taken, KDIR * NCH)
                for j in range(NCH):
                    for h in range(2):
                        c = 2 * j + h
                        if c >= 2:
                            e.wait_ge(z_act, c - 1)
                        mm(bank(4 + h), WZ2[:, ch(h, P)], xn_mid(j)).then_inc(z_proj, 1)

                def mean(j):
                    if j >= 2:
                        e.wait_ge(y_cent, j - 1)
                    mm(bank(j % 2), cst["ones"], Y2[:, 0, ch(j)], True, False)
                    mm(bank(j % 2), cst["ones"], Y2[:, 1, ch(j)], False, True).then_inc(y_mean, 1)

                def variance(j):
                    e.wait_ge(y_sq, j + 1)
                    if j >= 2:
                        e.wait_ge(y_rstd, j - 1)
                    mm(bank(2 + j % 2), cst["ones"], Q2[j % 2][:, 0, :], True, False)
                    mm(bank(2 + j % 2), cst["ones"], Q2[j % 2][:, 1, :], False, True).then_inc(y_var, 1)

                def project(j):
                    e.wait_ge(y_gated, j + 1)
                    if j >= 2:
                        e.wait_ge(x_added, 2 * NCH + j - 1)
                    mm(bank(6 + j % 2), WO2[:, 0:P], Y2[:, 0, ch(j)], True, False)
                    mm(bank(6 + j % 2), WO2[:, P:2 * P], Y2[:, 1, ch(j)], False, True).then_inc(y_out, 1)
                mean(0)
                for j in range(NCH):
                    if j + 1 < NCH:
                        mean(j + 1)
                    variance(j)
                    if j:
                        project(j - 1)
                project(NCH - 1)

            def block3():
                for j in range(NCH):
                    if j >= 2:
                        e.wait_ge(c3_act, j - 1)
                    for t in range(9):
                        r = mm(bank(j % 2), TAP3[:, ch(t, P)], xn_tap(j, t), t == 0, t == 8)
                    r.then_inc(c3_done, 1)
                e.wait_ge(pad3, 1)
                for j in range(NCH):
                    e.wait_ge(c3_act, j + 1)
                    if j >= 2:
                        e.wait_ge(u3_act, j - 1)
                    for t in range(3):
                        r = mm(bank(2 + j % 2), TAPU3[:, ch(t, P)], X1[:, NT * j + t:NT * j + t + NT], t == 0, t == 2)
                    r.then_inc(u3_proj, 1)
                for j in range(NCH):
                    if j >= 2:
                        e.wait_ge(z3_act, j - 1)
                    mm(bank(4 + j % 2), WZ3[:, :], X1[:, NT * j + 2:NT * j + 2 + NT]).then_inc(z3_proj, 1)
                e.wait_ge(u3_act, NCH)
                for j in range(NCH):
                    e.wait_ge(z3_act, NCH if j < 2 else NCH + j - 1)
                    mm(bank(4 + j % 2), W23[:, :], xn_mid(j)).then_inc(z3_proj, 1)
                e.wait_ge(z3_act, 2 * NCH)
                scan(S3)

                def project(j):
                    e.wait_ge(g3_gated, j + 1)
                    return mm(bank(j % 2), WO3[:, :], Y3[:, ch(j)])
                e.wait_ge(S3.y_taken, NCH)
                tail(2, project)
                for j in range(NCH):
                    e.wait_ge(g3_fused, j + 1)
                    if j >= 2:
                        e.wait_ge(x_added, 3 * NCH + j - 1)
                    mm(bank(4 + j % 2), WOUT3[:, :], Y3[:, ch(j)]).then_inc(g3_out, 1)

            e.wait_ge(weights_in, NLOADS)
            e.wait_ge(vec_setup, 1)
            mm(bank(7)[:, 0:1], cst["cen"], vec["b_out"])
            mm(bank(7)[:, 1:2], cst["cen"], vec["ffb1"]).then_inc(pe_setup, 1)
            e.wait_ge(vec_ready, 1)
            with e.Fori(0, B) as b:
                for layer, run in enumerate((block0, block1, block2, block3)[:LAYERS]):
                    group_norm(layer)
                    run()
                meet(e, b)

        @block.scalar
        def _(e):
            chain = [0]
            chain_sem = [act_setup]

            def act(o, i, f, **k):
                return nc.scalar.activation(o, i, f, **k)

            def link(ins):
                chain[0] += 1
                ins.then_inc(chain_sem[0], 1)
                e.wait_ge(chain_sem[0], chain[0])

            def group_norm(layer):
                e.wait_ge(gn_gvar, layer + 1)
                link(act(SM[:, 6:7], bank(7)[:, 1:2], ACT.Ln, bias=vec["eps"]))
                act(SM[:, 7:8], SM[:, 6:7], ACT.Exp, scale=-0.5).then_inc(gn_rstd, 1)

            def tail(layer, bias):
                base = NCH * layer

                def rstd(j):
                    e.wait_ge(t_var, base + j + 1)
                    if base + j:
                        e.wait_ge(t_rstd, base + j)
                    link(act(LV, bank(2 + j % 2), ACT.Ln, bias=vec["eps"]))
                    if j >= 2:
                        e.wait_ge(x_added, base + j - 1)
                    act(RS[j % 2], LV, ACT.Exp, scale=-0.5).then_inc(t_rstd, 1)
                for j in range(NCH):
                    e.wait_ge(t_proj, base + j + 1)
                    if j >= 2:
                        e.wait_ge(t_var, base + j - 1)
                    act(SQ[j % 2], bank(j % 2), ACT.Square, bias=bias).then_inc(t_sq, 1)
                    if j:
                        rstd(j - 1)
                rstd(NCH - 1)

            def block0():
                for j in range(NCH):
                    e.wait_ge(k_proj, j + 1)
                    act(KC[:, ch(j)], bank(j % 2), ACT.Copy).then_inc(k_copied, 1)
                for g in range(2 * NCH):
                    e.wait_ge(q_shifted, g + 1)
                    act(w3(VT[:, ch(g, 256)], a=2), w3(bank(2 + g % 4), a=2)[:, :, P:2 * P], ACT.Copy).then_inc(v_copied, 1)
                e.wait_ge(k_shift, 1)
                e.wait_ge(k_copied, NCH)
                act(KC, KC, ACT.Exp, bias=KMX[:, 9:10], accum_out=KMX[:, 10:11]).then_inc(k_exp, 1)
                for i in range(4):
                    e.wait_ge(q_shifted, 4 * i + 4)
                    act(QT[:, ch(i, 1024)], QT[:, ch(i, 1024)], ACT.Exp).then_inc(q_exp, 1)
                for g in range(NCH):
                    e.wait_ge(qT_made, g + 1)
                    act(QC[:, ch(g)], bank(2 + g % 2), ACT.Copy).then_inc(qT_copied, 1)
                tail(0, vec["b_out_c"])

            def block1():
                def spectra(x, q):
                    c = 4 * x + q
                    e.wait_ge(f_specp, 2 * c + 2)
                    ps = bank(2 + q % 2).rearrange("p (t y i r) -> p i y t r", t=8, i=2, r=2)[:, 1]
                    o = S1[x][:, :, 0, :]
                    if x == 0:
                        o = o.rearrange("p y (t r) -> p y t r", r=2)[:, :, 8 * q:8 * q + 8, :]
                    else:
                        o = o.rearrange("p y (r t) -> p y t r", r=2)[:, :, 8 * q:8 * q + 8, :]
                    act(o, ps, ACT.Copy, scale=-1.0).then_inc(f_specn, 1)
                for x in range(2):
                    for q in range(4):
                        spectra(x, q)
                for x in range(2):
                    for q in range(4):
                        c = 4 * x + q
                        e.wait_ge(f_mix, c + 1)
                        o = FS[x].rearrange("p (m y) -> p y m", y=2 * MODES)[:, 8 * q:8 * q + 8, :]
                        act(o, w3(bank(4 + q % 2), a=8), ACT.Copy).then_inc(f_mixc, 1)
                for x in range(2):
                    for q in range(4):
                        e.wait_ge(f_mixT, 4 * x + q + 1)
                        act(FT[x][:, ch(q)], bank(q % 2), ACT.Copy).then_inc(f_mixTc, 1)

                def relu(j):
                    for f in range(2):
                        e.wait_ge(h_proj, 4 * j + f + 1)
                        if j >= 2:
                            e.wait_ge(t_proj, NCH + j - 1)
                        act(H1[j % 2][:, ch(f)], bank(4 + f), ACT.Relu, bias=vec[f"ffb0_{f}"]).then_inc(h_reluA, 1)
                base = NCH

                def square(j):
                    e.wait_ge(t_proj, base + j + 1)
                    if j >= 2:
                        e.wait_ge(t_var, base + j - 1)
                    act(SQ[j % 2], bank(j % 2), ACT.Square, bias=vec["ffb1_c"]).then_inc(t_sq, 1)

                def rstd(j):
                    e.wait_ge(t_var, base + j + 1)
                    if base + j:
                        e.wait_ge(t_rstd, base + j)
                    link(act(LV, bank(2 + j % 2), ACT.Ln, bias=vec["eps"]))
                    if j >= 2:
                        e.wait_ge(x_added, base + j - 1)
                    act(RS[j % 2], LV, ACT.Exp, scale=-0.5).then_inc(t_rstd, 1)
                relu(0)
                for j in range(NCH):
                    if j + 1 < NCH:
                        relu(j + 1)
                    square(j)
                    if j:
                        rstd(j - 1)
                rstd(NCH - 1)

            def scan(S):
                w, N = S.halves, S.states

                def split(k, c, par, part):
                    if part == 0:
                        after(e, S.rows_ready, 1, k, c, 1)
                        after(e, S.b_bcast, N, k, c, -N)
                        after(e, S.c_bcast, N, k, c, -N)
                        act(TB[par][0:96, :], bank(6)[0:96, :], ACT.Copy).then_inc(S.split_cast, 1)
                        act(S.R[96:96 + RANK, :], bank(6)[96:96 + RANK, :], ACT.Copy).then_inc(S.split_cast, 1)
                    else:
                        after(e, S.split_rest, 2, k, c, part)
                        act(TB[par][0:96, :], S.R[0:96, :], ACT.Copy).then_inc(S.split_cast, 1)

                def softplus(k, c, h):
                    own = lambda i: after(e, S.softplus, 6 * w, k, c, 6 * h + i)
                    bias = S.DTB[:, w * k + h:w * k + h + 1]
                    after(e, S.dt_raw, w, k, c, h + 1)
                    after(e, S.dt_steps, 4 * w, k, c, 4 * h)
                    act(S.TA, bank(7 - h), ACT.Abs, bias=bias).then_inc(S.softplus, 1)
                    own(1)
                    act(S.E, S.TA, ACT.Exp, scale=-1.0).then_inc(S.softplus, 1)
                    own(2)
                    act(S.TA, S.E, ACT.Identity, bias=vec["mhalf"], scale=1.0 / 3).then_inc(S.softplus, 1)
                    act(S.MK, S.E, ACT.Relu, bias=vec["edge"], scale=-1.0).then_inc(S.softplus, 1)
                    act(S.LE, S.E, ACT.Ln, bias=vec["one"]).then_inc(S.softplus, 1)
                    act(S.RL, bank(7 - h), ACT.Relu, bias=bias).then_inc(S.softplus, 1)

                def copy_b(k, c, n):
                    after(e, S.b_bcast, N, k, c, n + 1)
                    after(e, S.drive, N, k, c, n - 1)
                    act(S.Bs[n % 2], bank(4 + n % 2), ACT.Copy).then_inc(S.b_copied, 1)

                def body(k, c, par, prv, nxt):
                    for n in range(N):
                        if n + 1 < N:
                            copy_b(k, c, n + 1)
                        elif nxt:
                            copy_b(*nxt, 0)
                        if nxt and n == S.p_c1:
                            split(*nxt, 1 - par, 0)
                        if nxt and n == S.p_c2:
                            split(*nxt, 1 - par, 1)
                        if nxt and n == S.p_c3:
                            split(*nxt, 1 - par, 2)
                        if n == 0:
                            after(e, S.dt_steps, 4 * w, k, c, 4 * w)
                        after(e, S.scanned, N, k, c, n - 1)
                        for h in range(w):
                            col = (w * k + h) * N + n
                            r = act(S.A[n % 2][:, ch(h)], S.DT[par][:, ch(h)], ACT.Exp, scale=S.AN[:, col:col + 1])
                        r.then_inc(S.decay, 1)
                        if nxt and n in S.p_sp:
                            softplus(*nxt, S.p_sp.index(n))

                split(0, 0, 0, 0)
                split(0, 0, 0, 1)
                split(0, 0, 0, 2)
                for h in range(w):
                    softplus(0, 0, h)
                copy_b(0, 0, 0)
                S.chunks(e, body)

            def exp_and_log():
                e.preload_act_table_set("natural_log_exp_and_others")

            def block2():
                for j in range(NCH):
                    for h in range(2):
                        c = 2 * j + h
                        e.wait_ge(conv_done, c + 1)
                        act(BIG1[:, h * L + j * NT:h * L + (j + 1) * NT], bank(c % 4), ACT.Silu,
                            bias=vec[f"cb{h}"]).then_inc(conv_act, 1)
                exp_and_log()
                e.wait_ge(conv_act, 2 * NCH)
                scan(S2)
                e.wait_ge(S2.du_ready, KDIR * NCH)
                for j in range(NCH):
                    for h in range(2):
                        e.wait_ge(z_proj, 2 * j + h + 1)
                        act(Z2[:, h, ch(j)], bank(4 + h), ACT.Silu).then_inc(z_act, 1)
                exp_and_log()

                def square(j):
                    e.wait_ge(y_cent, j + 1)
                    if j >= 2:
                        e.wait_ge(y_var, j - 1)
                    act(Q2[j % 2], Y2[:, :, ch(j)], ACT.Square).then_inc(y_sq, 1)

                def rstd(j):
                    e.wait_ge(y_var, j + 1)
                    if j:
                        e.wait_ge(y_rstd, j)
                    link(act(LV2, bank(2 + j % 2), ACT.Ln, bias=vec["eps"], scale=0.5))
                    if j >= 2:
                        e.wait_ge(y_norm, j - 1)
                    act(R2[j % 2], LV2, ACT.Exp, scale=-0.5).then_inc(y_rstd, 1)
                square(0)
                for j in range(NCH):
                    if j + 1 < NCH:
                        square(j + 1)
                    rstd(j)

            def block3():
                for j in range(NCH):
                    e.wait_ge(c3_done, j + 1)
                    act(X1[:, 2 + j * NT:2 + (j + 1) * NT], bank(j % 2), ACT.Silu).then_inc(c3_act, 1)
                for j in range(NCH):
                    e.wait_ge(u3_proj, j + 1)
                    act(U3[:, ch(j)], bank(2 + j % 2), ACT.Silu, bias=vec["cb3"]).then_inc(u3_act, 1)
                for j in range(NCH):
                    e.wait_ge(z3_proj, j + 1)
                    act(Z3[:, ch(j)], bank(4 + j % 2), ACT.Silu).then_inc(z3_act, 1)
                for j in range(NCH):
                    e.wait_ge(z3_proj, NCH + j + 1)
                    act(X2G[:, ch(j)], bank(4 + j % 2), ACT.Silu).then_inc(z3_act, 1)
                exp_and_log()
                scan(S3)

                base = 2 * NCH

                def rstd(j):
                    e.wait_ge(t_var, base + j + 1)
                    if base + j:
                        e.wait_ge(t_rstd, base + j)
                    link(act(LV, bank(2 + j % 2), ACT.Ln, bias=vec["eps"]))
                    if j >= 2:
                        e.wait_ge(g3_fused, j - 1)
                    act(RS[j % 2], LV, ACT.Exp, scale=-0.5).then_inc(t_rstd, 1)
                for j in range(NCH):
                    e.wait_ge(t_proj, base + j + 1)
                    if j >= 2:
                        e.wait_ge(t_var, base + j - 1)
                    act(SQ[j % 2], bank(j % 2), ACT.Square).then_inc(t_sq, 1)
                    if j:
                        rstd(j - 1)
                rstd(NCH - 1)

            exp_and_log()
            e.wait_ge(weights_in, NLOADS)
            for t in (AN2, AN3):
                link(act(t[:, :], t[:, :], ACT.Exp))
                link(act(t[:, :], t[:, :], ACT.Copy, scale=-1.0))
            with e.Fori(0, B) as b:
                chain[0], chain_sem[0] = 0, act_chain
                for layer, run in enumerate((block0, block1, block2, block3)[:LAYERS]):
                    group_norm(layer)
                    run()
                e.wait_ge(t_rstd, 8)
                meet(e, b)

        @block.vector
        def _(e):
            chain = [0]
            chain_sem = [vec_setup]
            V = nc.vector

            def link(ins):
                chain[0] += 1
                ins.then_inc(chain_sem[0], 1)
                e.wait_ge(chain_sem[0], chain[0])

            def group_norm(layer):
                if layer == 0:
                    e.wait_ge(x_loaded, 16)
                else:
                    e.wait_ge(x_added, NCH * layer)
                for j in range(NCH):
                    r = V.bn_stats(GST[:, 6 * j:6 * j + 6], X[:, ch(j)])
                link(r)
                V.bn_aggr(SM[:, 0:2], GST[:, :]).then_inc(gn_stats, 1)
                e.wait_ge(gn_mean, layer + 1)
                link(V.tensor_copy(SM[:, 5:6], bank(7)[:, 0:1]))
                link(V.tensor_sub(SM[:, 2:3], SM[:, 0:1], SM[:, 5:6]))
                link(V.tensor_tensor(SM[:, 3:4], SM[:, 2:3], SM[:, 2:3], MUL))
                V.tensor_tensor(SM[:, 4:5], SM[:, 3:4], SM[:, 1:2], ADD).then_inc(gn_var, 1)
                e.wait_ge(gn_rstd, layer + 1)
                link(V.tensor_tensor(SM[:, 8:9], SM[:, 5:6], SM[:, 7:8], MUL))
                for h in range(2):
                    o, i = XNF[:, ch(h, L // 2)], X[:, ch(h, L // 2)]
                    if layer >= 2:
                        o = XN3[:, 1 + 32 * h:33 + 32 * h, 1:1 + HW]
                        i = i.rearrange("p (h w) -> p h w", w=HW)
                    V.tensor_scalar(o, i, SM[:, 7:8], SM[:, 8:9], MUL, SUB).then_inc(xn_ready, 1)

            def tail(layer, bias, g, b):
                for j in range(NCH):
                    e.wait_ge(t_rstd, NCH * layer + j + 1)
                    t = RS[j % 2]
                    V.scalar_tensor_tensor(t, bank(j % 2), bias, t, ADD, MUL).then_inc(t_norm, 1)
                    e.wait_ge(t_norm, NCH * layer + j + 1)
                    link(V.tensor_scalar(t, t, g, b, MUL, ADD))
                    V.tensor_tensor(X[:, ch(j)], X[:, ch(j)], t, ADD).then_inc(x_added, 1)

            def block0():
                for j in range(NCH):
                    e.wait_ge(k_copied, j + 1)
                    V.reduce_max(KMX[:, j:j + 1], KC[:, ch(j)], AXX).then_inc(k_max, 1)
                e.wait_ge(k_max, NCH)
                link(V.reduce_max(KMX[:, 8:9], KMX[:, 0:8], AXX))
                V.tensor_scalar(KMX[:, 9:10], KMX[:, 8:9], -1.0, None, MUL).then_inc(k_shift, 1)
                for g in range(2 * NCH):
                    e.wait_ge(qv_proj, g + 1)
                    q = bank(2 + g % 4).rearrange("p (t c) -> p t c", t=2)[:, :, 0:P].rearrange("p t (h d) -> p t h d", d=DH)
                    m = QMX[:, 8 * g:8 * g + 8].rearrange("p (t h) -> p t h", t=2)
                    link(V.reduce_max(m, q, AXX))
                    V.tensor_tensor(QT[:, ch(g, 256)].rearrange("p (t h d) -> p t h d", t=2, d=DH), q,
                                    m.unsqueeze(3).to_broadcast([P, 2, HEADS, DH]), SUB).then_inc(q_shifted, 1)
                for i in range(4):
                    e.wait_ge(q_exp, i + 1)
                    q = QT[:, ch(i, 1024)].rearrange("p (a d) -> p a d", d=DH)
                    s = QS[:, ch(i, 32)]
                    link(V.reduce_sum(s, q, AXX))
                    link(V.reciprocal(s, s))
                    V.tensor_tensor(q, q, s.unsqueeze(2).to_broadcast([P, 32, DH]), MUL).then_inc(q_norm, 1)
                for g in range(NCH):
                    e.wait_ge(kT_made, g + 1)
                    V.tensor_copy(KT[:, ch(g)], bank(g % 2)).then_inc(kT_copied, 1)
                e.wait_ge(ctx_made, 1)
                V.tensor_tensor(CT, bank(6)[:, 0:P], cst["head"], MUL).then_inc(ctx_masked, 1)
                e.wait_ge(k_exp, 1)
                link(V.reciprocal(KMX[:, 11:12], KMX[:, 10:11]))
                e.wait_ge(m2_made, 1)
                V.tensor_scalar(M2S, bank(6)[:, P:2 * P], KMX[:, 11:12], float(DH) ** -0.5, MUL, MUL).then_inc(m2_ready, 1)
                tail(0, vec["b_out_c"], vec["g0"], vec["b0"])

            def block1():
                for x in range(2):
                    def spectra(q):
                        c = 4 * x + q
                        e.wait_ge(f_spec, c + 1)
                        for im in range(2):
                            ps = bank(2 + q % 2).rearrange("p (t y i r) -> p i y t r", t=8, i=2, r=2)[:, im]
                            o = S1[x][:, :, 1 + im, :]
                            if x == 0:
                                o = o.rearrange("p y (t r) -> p y t r", r=2)[:, :, 8 * q:8 * q + 8, :]
                            else:
                                o = o.rearrange("p y (r t) -> p y t r", r=2)[:, :, 8 * q:8 * q + 8, :]
                            V.tensor_copy(o, ps).then_inc(f_specp, 1)
                    for g in range(NCH):
                        c = NCH * x + g
                        e.wait_ge(f_trans, c + 1)
                        if g % 2 == 0 and c:
                            pass
                        if c >= 2:
                            e.wait_ge(f_trans, c + 1)
                        V.tensor_copy(XT[g % 2], bank(g % 2)).then_inc(f_transc, 1)
                        if g % 2 == 0 and g:
                            spectra(g // 2 - 1)
                    spectra(3)
                for x in range(2):
                    for j in range(NCH):
                        e.wait_ge(f_inv, NCH * x + j + 1)
                        if x == 0:
                            V.tensor_copy(HF[:, ch(j)], bank(2 + j % 2)).then_inc(f_sum, 1)
                        else:
                            if j == 0:
                                e.wait_ge(f_sum, NCH)
                            h = HF.rearrange("p (m n) -> p n m", n=HW)[:, ROWS * j:ROWS * (j + 1), :]
                            V.tensor_tensor(h, h, w3(bank(2 + j % 2), a=ROWS), ADD).then_inc(f_sum, 1)

                def relu(j):
                    for f in range(2, 4):
                        e.wait_ge(h_proj, 4 * j + f + 1)
                        if j >= 2:
                            e.wait_ge(t_proj, NCH + j - 1)
                        V.tensor_scalar(H1[j % 2][:, ch(f)], bank(4 + f), vec[f"ffb0_{f}"], 0.0, ADD, MAX).then_inc(h_reluV, 1)
                relu(0)
                for j in range(NCH):
                    if j + 1 < NCH:
                        relu(j + 1)
                    e.wait_ge(t_rstd, NCH + j + 1)
                    t = RS[j % 2]
                    V.scalar_tensor_tensor(t, bank(j % 2), vec["ffb1_c"], t, ADD, MUL).then_inc(t_norm, 1)
                    e.wait_ge(t_norm, NCH + j + 1)
                    link(V.tensor_scalar(t, t, vec["g1"], vec["b1"], MUL, ADD))
                    V.tensor_tensor(X[:, ch(j)], X[:, ch(j)], t, ADD).then_inc(x_added, 1)

            def scan(S):
                w, N = S.halves, S.states

                def rest(k, c, par, part):
                    after(e, S.split_cast, 4, k, c, 3 if part else 1)
                    src = bank(6)[0:96, :] if part == 0 else S.R[0:96, :]
                    V.scalar_tensor_tensor(S.R[0:96, :], TB[par][0:96, :], cst["m1" if part == 0 else "m2"][0:96, :],
                                           src, MUL, ADD).then_inc(S.split_rest, 1)

                def make_dt(k, c, par, h):
                    own = lambda i: after(e, S.dt_steps, 4 * w, k, c, 4 * h + i)
                    after(e, S.softplus, 6 * w, k, c, 6 * h + 6)
                    V.tensor_tensor(S.TA, S.TA, S.E, MUL).then_inc(S.dt_steps, 1)
                    own(1)
                    V.scalar_tensor_tensor(S.TA, S.TA, 1.0, S.E, ADD, MUL).then_inc(S.dt_steps, 1)
                    own(2)
                    V.memset(SM[:, 12:13], 0.0)
                    V.copy_predicated(S.LE, S.MK.bitcast(mybir.dt.uint32), S.TA).then_inc(S.dt_steps, 1)
                    own(3)
                    after(e, S.decay, N, k, c, -N)
                    V.tensor_tensor(S.DT[par][:, ch(h)], S.LE, S.RL, ADD).then_inc(S.dt_steps, 1)

                def take_y(k, c):
                    after(e, S.summed, N, k, c, N)
                    pos = S.position(k, c)
                    y = S.cols(BIG2, S.y0, k, pos)
                    if k == 0:
                        u = S.cols(BIG1, S.u0, k, pos)
                        for h in range(w):
                            dd = vec[f"Dt{h}" if w == 2 else "Dp3"]
                            r = V.scalar_tensor_tensor(y[:, h], u[:, h], dd, bank(h), MUL, ADD)
                        r.then_inc(S.y_taken, 1)
                    else:
                        if k == 1:
                            after(e, S.y_taken, 1, k, 0, 0)
                        ps = PS[:, 0:w, :]
                        if k % 2:
                            ps = ps.rearrange("p d (w h) -> p d w h", h=HW)
                        V.tensor_tensor(y, y, ps, ADD).then_inc(S.y_taken, 1)

                def states(k, c, n):
                    after(e, S.decay, N, k, c, n + 1)
                    after(e, S.drive, N, k, c, n + 1)
                    after(e, S.carried, N, k, c, n + 1 - N)
                    q = S.Bq[n % 4]
                    for h in range(w):
                        a, b = S.A[n % 2][:, ch(h)], q[:, ch(h)]
                        if k >= 2:
                            a, b = a[:, ::-1], b[:, ::-1]
                        first = k == 0 and isinstance(c, int) and c == 0
                        r = V.tensor_tensor_scan(b, a, b, 0.0 if first else S.HST[:, w * n + h:w * n + h + 1], MUL, ADD)
                    r.then_inc(S.scanned, 1)

                def body(k, c, par, prv, nxt):
                    rev = k >= 2
                    for n in range(N):
                        q = S.Bq[n % 4]
                        after(e, S.scanned, N, k, c, n + 1)
                        last = 0 if rev else NT - 1
                        ends = q.rearrange("p (d l) -> p d l", l=NT)[:, :, last]
                        if isinstance(c, int) and c == NCH - 1:
                            V.memset(S.HST[:, w * n:w * n + w], 0.0).then_inc(S.carried, 1)
                        else:
                            V.tensor_copy(S.HST[:, w * n:w * n + w], ends).then_inc(S.carried, 1)
                        if n + 1 < N:
                            states(k, c, n + 1)
                        elif nxt:
                            states(*nxt, 0)
                        after(e, S.c_bcast, N, k, c, n + 1)
                        after(e, S.carried, N, k, c, n + 1)
                        qv = q.rearrange("p (d l) -> p d l", l=NT)
                        V.tensor_tensor(qv, qv, bank(2 + n % 2).unsqueeze(1).to_broadcast([P, w, NT]), MUL)\
                            .then_inc(S.weighed, 1)
                        if n == 0 and prv:
                            take_y(*prv)
                        if nxt and n == S.p_r1:
                            rest(*nxt, 1 - par, 0)
                        if nxt and n == S.p_r2:
                            rest(*nxt, 1 - par, 1)
                        if nxt and n in S.p_cb:
                            make_dt(*nxt, 1 - par, S.p_cb.index(n))

                rest(0, 0, 0, 0)
                rest(0, 0, 0, 1)
                for h in range(w):
                    make_dt(0, 0, 0, h)
                states(0, 0, 0)
                S.chunks(e, body)
                take_y(S.dirs - 1, NCH - 1)

            def block2():
                scan(S2)
                e.wait_ge(S2.y_taken, KDIR * NCH)

                def centre(j):
                    e.wait_ge(y_mean, j + 1)
                    y = Y2[:, :, ch(j)]
                    for h in range(2):
                        r = V.scalar_tensor_tensor(Y2[:, h, ch(j)], bank(j % 2), -0.5, Y2[:, h, ch(j)], MUL, ADD)
                    r.then_inc(y_cent, 1)

                def add(j):
                    e.wait_ge(y_out, j + 1)
                    V.tensor_tensor(X[:, ch(j)], X[:, ch(j)], bank(6 + j % 2), ADD).then_inc(x_added, 1)
                centre(0)
                for j in range(NCH):
                    if j + 1 < NCH:
                        centre(j + 1)
                    e.wait_ge(y_rstd, j + 1)
                    e.wait_ge(y_sq, j + 1)
                    y = Y2[:, :, ch(j)]
                    link(V.tensor_tensor(y, y, R2[j % 2].unsqueeze(1).to_broadcast([P, 2, NT]), MUL))
                    for h in range(2):
                        r = V.tensor_scalar(Y2[:, h, ch(j)], Y2[:, h, ch(j)], vec[f"ng{h}"], vec[f"nb{h}"], MUL, ADD)
                    r.then_inc(y_norm, 1)
                    if j:
                        add(j - 1)
                add(NCH - 1)

            def block3():
                scan(S3)
                for j in range(NCH):
                    e.wait_ge(t_rstd, 2 * NCH + j + 1)
                    t = RS[j % 2]
                    V.tensor_tensor(t, bank(j % 2), t, MUL).then_inc(t_norm, 1)
                    e.wait_ge(t_norm, 2 * NCH + j + 1)
                    link(V.tensor_scalar(t, t, vec["gam3"], vec["bet3"], MUL, ADD))
                    e.wait_ge(z3_act, 2 * NCH)
                    V.tensor_tensor(Y3[:, ch(j)], t, X2G[:, ch(j)], MUL).then_inc(g3_fused, 1)
                for j in range(NCH):
                    e.wait_ge(g3_out, j + 1)
                    V.tensor_tensor(X[:, ch(j)], X[:, ch(j)], bank(4 + j % 2), ADD).then_inc(x_added, 1)

            e.wait_ge(weights_in, NLOADS)
            def centre_rows(t):
                link(V.reduce_sum(SM[:, 10:11], t, AXX))
                link(V.tensor_scalar(SM[:, 11:12], SM[:, 10:11], -1.0 / P, None, MUL))
                link(V.tensor_scalar(t, t, SM[:, 11:12], None, ADD))
            for t in [WO0[:, :], WO3[:, :]] + [FW1[:, ch(f, P)] for f in range(4)]:
                centre_rows(t)
            V.tensor_copy(w3(SEL[:, :], a=32), cst["onehot"].unsqueeze(2).to_broadcast([P, 32, P]))
            for h in range(2):
                link(V.tensor_tensor(vec[f"Dt{h}"], vec[f"D{h}"], vec[f"D{h + 2}"], ADD))
                link(V.tensor_tensor(vec[f"Dt{h}"], vec[f"Dt{h}"], vec[f"D{h + 4}"], ADD))
                link(V.tensor_tensor(vec[f"Dt{h}"], vec[f"Dt{h}"], vec[f"D{h + 6}"], ADD))
            for t, wt, n in ((TAP2, BIG1[:, 0:256], 9), (TAP3, BD1[:, :], 9), (TAPU3, WU3[:, :], 3)):
                wide = wt.unsqueeze(1).to_broadcast([P, n, wt.shape[1]])
                link(V.tensor_tensor(w3(t[:, :], a=n), w3(t[:, :], a=n), wide, MUL))
            e.wait_ge(pe_setup, 1)
            link(V.tensor_copy(vec["b_out_c"], bank(7)[:, 0:1]))
            V.tensor_copy(vec["ffb1_c"], bank(7)[:, 1:2]).then_inc(vec_ready, 1)
            e.wait_ge(vec_ready, 1)
            with e.Fori(0, B) as b:
                chain[0], chain_sem[0] = 0, dve_chain
                for layer, run in enumerate((block0, block1, block2, block3)[:LAYERS]):
                    group_norm(layer)
                    run()
                e.wait_ge(x_added, NCH * LAYERS)
                meet(e, b)


def kernel(**inputs):
    import concourse.bacc as _bacc
    from concourse.bass_utils import run_bass_kernel_spmd as _run

    a = {n: np.asarray(v) for n, v in inputs.items()}
    x = a["x"]
    B = x.shape[0]
    col = lambda v: v.reshape(P, 1)
    q, k, v = np.split(a["L0_conv_w_qkv"], 3, axis=1)
    Ds = a["L2_conv_Ds"].reshape(KDIR * 2, P)
    fill = lambda c: np.full((P, 1), c, np.float32)
    cols = [a["L0_conv_b_out"], fill(0), a["L0_conv_g_ln"], a["L0_conv_b_ln"], a["L1_conv_ff_b1"], fill(0),
            a["L1_conv_ln_g"], a["L1_conv_ln_b"], *a["L1_conv_ff_b0"].reshape(4, P),
            *a["L2_conv_conv_b"].reshape(2, P), *a["L2_conv_norm_g"].reshape(2, P), *a["L2_conv_norm_b"].reshape(2, P),
            *Ds, fill(0), fill(0), a["L3_conv_conv1d_b"], a["L3_conv_D_param"], a["L3_conv_gamma"], a["L3_conv_beta"],
            fill(1e-5), fill(1), fill(-0.5), fill(1 / 128)]
    xp = a["L2_conv_x_proj_w"].reshape(KDIR, RANK + 2 * SN, 2, P).transpose(3, 0, 2, 1)
    xp3 = a["L3_conv_x_proj_w"].T
    ip2, ip3 = a["L2_conv_in_proj_w"].T, a["L3_conv_in_proj_w"].T
    halves = lambda w: w.reshape(*w.shape[:-1], 2, P)
    weights = {
        "vecs": np.concatenate([col(c) for c in cols], 1),
        "wk": k, "wqv": np.concatenate([q, v], 1), "wo0": a["L0_conv_w_out"],
        "spec1": a["L1_conv_w1"].transpose(0, 2, 3, 1).reshape(P, -1),
        "spec2": a["L1_conv_w2"].transpose(0, 2, 3, 1).reshape(P, -1),
        "ffw0": a["L1_conv_ff_w0"], "ffw1": a["L1_conv_ff_w1"].reshape(4, P, P).transpose(1, 0, 2),
        "inpx": ip2[:, :2 * P], "inpz": ip2[:, 2 * P:],
        "cw2": a["L2_conv_conv_w"].reshape(2 * P, 9).T.reshape(-1),
        "wo2": a["L2_conv_out_proj_w"].T.reshape(2, P, P).transpose(1, 0, 2).reshape(P, -1),
        "dtw2": a["L2_conv_dt_proj_w"].transpose(2, 0, 1).reshape(RANK, -1),
        "dtb2": a["L2_conv_dt_proj_b"].reshape(KDIR * 2, P).T,
        "al2": a["L2_conv_A_logs"].reshape(KDIR * 2, P, SN).transpose(1, 0, 2).reshape(P, -1),
        "xdt2": xp[..., :RANK], "xbc2": xp[..., RANK:],
        "dw3": a["L3_conv_dw"].reshape(-1), "inpu3": ip3[:, :P], "inpz3": ip3[:, P:],
        "cw3": a["L3_conv_conv1d_w"].T.reshape(-1), "dtw3": a["L3_conv_dt_proj_w"].T,
        "dtb3": col(a["L3_conv_dt_proj_b"]), "al3": a["L3_conv_A_log"], "wo3": a["L3_conv_out_proj_w"].T,
        "xdt3": xp3[:, :RANK], "xbc3": xp3[:, RANK:],
        "w1": a["L3_conv_w1"].transpose(0, 2, 1), "w2": a["L3_conv_w2"].transpose(0, 2, 1),
        "wout": a["L3_conv_wout"].transpose(0, 2, 1),
    }
    nc = _bacc.Bacc("TRN2", target_bir_lowering=False, num_devices=1)
    arrays, handles = {}, {}
    sources = {"x": x.reshape(B, L, P).transpose(0, 2, 1), "consts": shape_constants(), **weights}
    for name, value in sources.items():
        value = np.ascontiguousarray(value)
        arrays[f"in_{name}_dram"] = value
        handles[name] = nc.dram_tensor(f"in_{name}_dram", value.shape, mybir.dt.from_np(value.dtype), kind="ExternalInput").ap()
    out = nc.dram_tensor("out_0_dram", (B, P, L), mybir.dt.float32, kind="ExternalOutput").ap()
    program(nc, handles["x"], handles["consts"], {n: handles[n] for n in weights}, out)
    r = _run(nc, [arrays], core_ids=[0])
    return np.ascontiguousarray(r.results[0]["out_0_dram"].transpose(0, 2, 1)).reshape(x.shape)
```

```python
import numpy as np
import concourse.bass as bass
from concourse import mybir
from contextlib import ExitStack

LAYERS = 4
P = 128
HW = 64
L = HW * HW
NT = 512
NCH = L // NT
ROWS = NT // HW
PW = HW + 2
MODES = 16
HEADS, DH = 4, 32
KDIR = 4
SN = 16
SN3 = 8
RANK = 8
GROUPS = 32


def shape_constants():
    f = np.float32
    eye = np.eye(P, dtype=f)
    cen = eye - f(1.0 / P)
    ones = np.full((P, P), 1.0 / P, f)
    grp = np.kron(np.eye(GROUPS), np.full((P // GROUPS,) * 2, GROUPS / P)).astype(f)
    head = np.kron(np.eye(HEADS), np.ones((DH, DH))).astype(f)
    y, w = np.arange(MODES), np.arange(HW)
    ang = 2 * np.pi * np.outer(w, y) / HW
    fwd = np.stack([np.cos(ang), -np.sin(ang)], 2) / np.sqrt(HW)
    fw = np.zeros((2, HW, MODES, 2, 2)); fh = np.zeros((HW, 2, MODES, 2, 2))
    for r in range(2):
        fw[r, :, :, :, r] = fwd
        fh[:, r, :, :, r] = fwd
    c = np.where(y == 0, 1.0, 2.0)[:, None] / np.sqrt(HW)
    inv = np.stack([c * np.cos(ang.T), -c * np.sin(ang.T)], 1)
    fi = np.zeros((4, MODES, 2, 4, HW))
    for m in range(4):
        fi[m, :, :, m, :] = inv
    onehot = np.zeros((P, 32)); onehot[np.arange(96), np.arange(96) % 32] = 1
    m1 = np.zeros((P, 1)); m1[32:96] = -1
    m2 = np.zeros((P, 1)); m2[64:96] = -1
    return np.concatenate([eye, cen, ones, grp, head, fw.reshape(P, 64), fh.reshape(P, 64),
                           fi.reshape(P, 256), onehot, m1, m2], 1).astype(f)


CONST_COLS = {}
_at = 0
for _n, _w in (("eye", P), ("cen", P), ("ones", P), ("grp", P), ("head", P), ("fw", 64), ("fh", 64),
               ("fi", 256), ("onehot", 32), ("m1", 1), ("m2", 1)):
    CONST_COLS[_n] = (_at, _at + _w)
    _at += _w
NCONST = _at


def program(nc, x_in, consts, d, out):
    fp32, bf16 = mybir.dt.float32, mybir.dt.bfloat16
    ALU, ACT, AXX = mybir.AluOpType, mybir.ActivationFunctionType, mybir.AxisListType.X
    MUL, ADD, SUB, MAX = ALU.mult, ALU.add, ALU.subtract, ALU.max
    B = x_in.shape[0]
    ctx = ExitStack()
    with ctx:
        def sb(name, cols, dt=fp32):
            return ctx.enter_context(nc.sbuf_tensor(name, [P, cols], dt))

        persistent = []

        def sem(name):
            s = ctx.enter_context(nc.semaphore(name))
            return s

        def sample_sem(name):
            s = sem(name)
            persistent.append(s)
            return s

        X = sb("X", L)
        XN = sb("XN", PW * PW)
        BIG1 = sb("BIG1", 2 * L + 8)
        BIG2 = sb("BIG2", 2 * L)
        WORK = sb("WORK", 15360)
        CST = sb("CST", NCONST)
        WK = sb("WK", P); WQV = sb("WQV", 2 * P); WO0 = sb("WO0", P)
        FW0 = sb("FW0", 4 * P); FW1 = sb("FW1", 4 * P)
        WZ2 = sb("WZ2", 2 * P); WX1 = sb("WX1", P); TAP2 = sb("TAP2", 9 * P); TC2 = sb("TC2", 9); WO2 = sb("WO2", 2 * P)
        XP2 = sb("XP2", KDIR * 2 * 104); DTW2 = sb("DTW2", KDIR * 2 * P)
        DTB2 = sb("DTB2", KDIR * 2); AN2 = sb("AN2", KDIR * 2 * SN)
        TAP3 = sb("TAP3", 9 * P); TAPU3 = sb("TAPU3", 3 * P)
        WZ3 = sb("WZ3", P); XP3 = sb("XP3", 104); DTW3 = sb("DTW3", P); DTB3 = sb("DTB3", 1)
        AN3 = sb("AN3", SN3); WO3 = sb("WO3", P); W23 = sb("W23", P); WOUT3 = sb("WOUT3", P)
        SEL = sb("SEL", 32 * P, bf16)
        VEC = sb("VEC", 40)
        SM = sb("SM", 32)
        GST = sb("GST", NCH * 6)
        HST2 = sb("HST2", 2 * SN); HST3 = sb("HST3", SN3)

        names = ["b_out", "b_out_c", "g0", "b0", "ffb1", "ffb1_c", "g1", "b1", "ffb0_0", "ffb0_1", "ffb0_2",
                 "ffb0_3", "cb0", "cb1", "ng0", "ng1", "nb0", "nb1", "D0", "D1", "D2", "D3", "D4", "D5", "D6",
                 "D7", "Dt0", "Dt1", "cb3", "Dp3", "gam3", "bet3", "eps", "one", "series", "edge"]
        vec = {n: VEC[:, i:i + 1] for i, n in enumerate(names)}
        vcol = {n: i for i, n in enumerate(names)}
        cst = {n: CST[:, a:b] for n, (a, b) in CONST_COLS.items()}
        EYE = cst["eye"]

        PS = ctx.enter_context(nc.psum_tensor("PS", [P, 8, NT], fp32))

        def bank(i):
            return PS[:, i, :]

        XNF = XN[:, 0:L]
        XN3 = XN[:, :].rearrange("p (h w) -> p h w", w=PW)

        def xn_tap(j, t):
            r, c = ROWS * j + t // 3, t % 3
            return XN3[:, r:r + ROWS, c:c + HW]

        def xn_mid(j):
            return xn_tap(j, 4)

        def ch(j, w=NT):
            return slice(j * w, (j + 1) * w)

        KC = BIG1[:, 0:L]
        KT = BIG1[:, L:2 * L]
        VT = WORK[:, 0:L]
        QT = WORK[:, L:2 * L]
        QC = WORK[:, 2 * L:3 * L]
        L0S = sb("L0S", 4 * P + 16)
        CT, M2S, QS, QMX = (L0S[:, P * i:P * i + P] for i in range(4))
        KMX = L0S[:, 4 * P:4 * P + 12]
        T0 = 3 * L
        SQ = [WORK[:, T0 + NT * i:T0 + NT * (i + 1)] for i in range(2)]
        RS = [WORK[:, T0 + NT * i:T0 + NT * (i + 1)] for i in (2, 3)]
        LV = WORK[:, T0 + 4 * NT:T0 + 5 * NT]
        SPEC = BIG2[:, :].rearrange("p (x y r o) -> p x y r o", x=2, y=MODES, r=2)
        HF = BIG1[:, 0:L]
        XT = [WORK[:, NT * i:NT * (i + 1)] for i in range(2)]
        S1 = [a.rearrange("p (y b m) -> p y b m", y=MODES, b=3)
              for a in (BIG1[:, L:L + 3 * 1024], WORK[:, 1024:4096])]
        FS = [WORK[:, L + 2048 * i:L + 2048 * (i + 1)] for i in range(2)]
        FT = [WORK[:, 2 * L + 2048 * i:2 * L + 2048 * (i + 1)] for i in range(2)]
        H1 = [WORK[:, 2048 * i:2048 * (i + 1)] for i in range(2)]
        TB = [sb(f"TB{i}", NT, bf16) for i in range(2)]

        class Scan:

            def __init__(s, tag, halves, states, dirs, at, u0, y0, xp, dtw, dtb, an, hst):
                s.halves, s.states, s.dirs, s.ahead = halves, states, dirs, not at
                if at:
                    (s.p_xp, s.p_c1, s.p_r1, s.p_c2, s.p_r2, s.p_c3, s.p_dt, s.p_sp, s.p_cb, s.p_sum, s.p_du) = at
                w = halves * NT
                at_col = [0]

                def take(n):
                    at_col[0] += n
                    return WORK[:, at_col[0] - n:at_col[0]]
                s.A = [XN[:, w * i:w * (i + 1)] for i in range(4)]
                order = [n % 5 for n in range(15)] + [5] if states == 16 else list(range(states))
                bufs = [take(w) for _ in range(max(order) + 1)]
                s.Bq = [bufs[i] for i in order]
                s.back = [next(m for m in range(1, states + 1) if order[n - m] == order[n]) for n in range(states)]
                s.DT = take(L) if s.ahead else [take(w) for _ in range(2)]
                s.DU = BIG2[:, y0:y0 + L] if s.ahead else [take(w) for _ in range(2)]
                s.TB = take(L // 2).bitcast(bf16) if s.ahead else [t[:, :] for t in TB]
                s.Bs = [take(NT) for _ in range(4)]
                s.R = take(NT)
                s.LE = take(w)
                s.TA, s.E, s.MK = (take(NT) for _ in range(3))
                s.u0, s.y0 = u0, y0
                s.XP, s.DTW, s.DTB, s.AN, s.HST = xp, dtw, dtb, an, hst
                s.rows_ready = sample_sem(tag + "_rows_ready")
                s.split_cast = sample_sem(tag + "_split_cast")
                s.split_rest = sample_sem(tag + "_split_rest")
                s.dt_raw = sample_sem(tag + "_dt_raw")
                s.softplus = sample_sem(tag + "_softplus")
                s.dt_steps = sample_sem(tag + "_dt_steps")
                s.dt_made = sample_sem(tag + "_dt_made")
                s.du_ready = sample_sem(tag + "_du_ready")
                s.b_bcast = sample_sem(tag + "_b_bcast")
                s.b_copied = sample_sem(tag + "_b_copied")
                s.c_bcast = sample_sem(tag + "_c_bcast")
                s.decay = sample_sem(tag + "_decay")
                s.drive = sample_sem(tag + "_drive")
                s.scanned = sample_sem(tag + "_scanned")
                s.carried = sample_sem(tag + "_carried")
                s.weighed = sample_sem(tag + "_weighed")
                s.summed = sample_sem(tag + "_summed")
                s.y_taken = sample_sem(tag + "_y_taken")

            def of(s, buf, c, par):
                return buf[:, c * NT:(c + 1) * NT] if s.ahead else buf[par]

            def cols(s, big, start, k, pos):
                v = big[:, start:start + s.halves * L]
                if k % 2 == 0:
                    return v.rearrange("p (d l) -> p d l", l=L)[:, :, bass.ds(pos * NT, NT)]
                return v.rearrange("p (d h w) -> p d w h", h=HW, w=HW)[:, :, bass.ds(pos * ROWS, ROWS), :]

            def like(s, ap, k):
                if k % 2 == 0:
                    return ap.rearrange("p (d l) -> p d l", l=NT)
                return ap.rearrange("p (d w h) -> p d w h", w=ROWS, h=HW)

            def position(s, k, c):
                return c if k < 2 else c * -1 + (NCH - 1)

            def chunks(s, e, body):
                def pair(k, c, before, after):
                    body(k, c, 0, before, (k, c + 1))
                    body(k, c + 1, 1, (k, c), after)
                if s.ahead:
                    for c in range(0, NCH, 2):
                        pair(0, c, (0, c - 1) if c else None, (0, c + 2) if c + 2 < NCH else None)
                    return
                for k in range(s.dirs):
                    pair(k, 0, (k - 1, NCH - 1) if k else None, (k, 2))
                    with e.Fori(1, NCH // 2 - 1) as i:
                        pair(k, 2 * i, (k, 2 * i - 1), (k, 2 * i + 2))
                    pair(k, NCH - 2, (k, NCH - 3), (k + 1, 0) if k + 1 < s.dirs else None)

        S2 = Scan("s2", 2, SN, KDIR, (0, 5, 3, 7, 5, 9, 3, (7, 11), (8, 11), (11, 14), 15), 0, 0, XP2, DTW2, DTB2, AN2, HST2)
        S3 = Scan("s3", 1, SN3, 1, None, L + 4, 0, XP3, DTW3, DTB3, AN3, HST3)

        def after(e, s, per_chunk, k, c, off):
            v = c * per_chunk + (k * NCH * per_chunk + off)
            if isinstance(v, int) and v <= 0:
                return
            e.wait_ge(s, v)

        BD1, WU3 = BIG1[:, 2 * P:3 * P], BIG1[:, 3 * P:4 * P]
        PX3 = WORK[:, 0:PW * PW].rearrange("p (h w) -> p h w", w=PW)
        DW = [WORK[:, PW * PW + NT * i:PW * PW + NT * (i + 1)] for i in range(2)]
        Z2 = BIG1[:, :2 * L].rearrange("p (d l) -> p d l", l=L)
        Y2 = BIG2[:, :].rearrange("p (d l) -> p d l", l=L)
        Q2 = [WORK[:, 1024 * i:1024 * (i + 1)].rearrange("p (d l) -> p d l", l=NT) for i in range(2)]
        R2 = [WORK[:, 2048 + NT * i:2048 + NT * (i + 1)] for i in range(2)]
        LV2 = WORK[:, 3072:3584]
        X1 = BIG1[:, 0:L + 2]
        X2G = BIG1[:, 0:L]
        U3 = BIG1[:, L + 4:2 * L + 4]
        GROUPS3 = [(0, 1), (2, 3), (4, 5), (6, 7)]
        Y3 = BIG2[:, 0:L]
        Z3 = BIG2[:, L:2 * L]

        weights_in = sem("weights_in"); zeroed = sem("zeroed"); vec_setup = sem("vec_setup")
        act_setup = sem("act_setup"); pe_setup = sem("pe_setup"); vec_ready = sem("vec_ready")
        sample_done = sem("sample_done"); next_sample = sem("next_sample")
        x_loaded = sample_sem("x_loaded"); spec_loaded = sample_sem("spec_loaded"); x_stored = sample_sem("x_stored")
        act_chain = sample_sem("act_chain"); dve_chain = sample_sem("dve_chain")
        gn_stats = sample_sem("gn_stats"); gn_mean = sample_sem("gn_mean"); gn_var = sample_sem("gn_var")
        gn_gvar = sample_sem("gn_gvar"); gn_rstd = sample_sem("gn_rstd"); xn_ready = sample_sem("xn_ready")
        frame_zero = sample_sem("frame_zero"); xn_again = sample_sem("xn_again")
        k_proj = sample_sem("k_proj"); k_copied = sample_sem("k_copied"); k_max = sample_sem("k_max")
        k_shift = sample_sem("k_shift"); k_exp = sample_sem("k_exp"); qv_proj = sample_sem("qv_proj")
        v_copied = sample_sem("v_copied"); q_shifted = sample_sem("q_shifted"); q_exp = sample_sem("q_exp")
        q_norm = sample_sem("q_norm"); kT_made = sample_sem("kT_made"); kT_copied = sample_sem("kT_copied")
        qT_made = sample_sem("qT_made"); qT_copied = sample_sem("qT_copied"); ctx_made = sample_sem("ctx_made")
        ctx_masked = sample_sem("ctx_masked"); m2_made = sample_sem("m2_made"); m2_ready = sample_sem("m2_ready")
        t_proj = sample_sem("t_proj"); t_sq = sample_sem("t_sq"); t_var = sample_sem("t_var")
        t_rstd = sample_sem("t_rstd"); t_norm = sample_sem("t_norm"); x_added = sample_sem("x_added")
        f_trans = sample_sem("f_trans"); f_transc = sample_sem("f_transc"); f_spec = sample_sem("f_spec")
        f_specn = sample_sem("f_specn"); f_specp = sample_sem("f_specp"); f_mix = sample_sem("f_mix")
        f_mixc = sample_sem("f_mixc"); f_mixT = sample_sem("f_mixT"); f_mixTc = sample_sem("f_mixTc")
        f_inv = sample_sem("f_inv"); f_sum = sample_sem("f_sum"); h_proj = sample_sem("h_proj")
        h_reluA = sample_sem("h_reluA"); h_reluV = sample_sem("h_reluV")
        conv_done = sample_sem("conv_done"); conv_act = sample_sem("conv_act")
        px_frame = sample_sem("px_frame"); px_made = sample_sem("px_made"); px_copied = sample_sem("px_copied")
        dw_done = sample_sem("dw_done"); dw_act = sample_sem("dw_act")
        z_proj = sample_sem("z_proj"); z_act = sample_sem("z_act")
        y_mean = sample_sem("y_mean"); y_cent = sample_sem("y_cent"); y_sq = sample_sem("y_sq")
        y_var = sample_sem("y_var"); y_rstd = sample_sem("y_rstd"); y_norm = sample_sem("y_norm")
        y_gated = sample_sem("y_gated"); y_out = sample_sem("y_out"); y_added = sample_sem("y_added")
        c3_done = sample_sem("c3_done"); c3_act = sample_sem("c3_act"); u3_proj = sample_sem("u3_proj")
        u3_act = sample_sem("u3_act"); g3_gated = sample_sem("g3_gated"); g3_fused = sample_sem("g3_fused")
        g3_out = sample_sem("g3_out"); pad3 = sample_sem("pad3"); z3_proj = sample_sem("z3_proj"); z3_act = sample_sem("z3_act")

        block = ctx.enter_context(nc.Block())

        w3 = lambda ap, **k: ap.rearrange("p (a b) -> p a b", **k)
        XP2v = XP2[:, :].rearrange("p (k d c) -> p k d c", k=KDIR, d=2)
        LOADS = [(CST[:, :], consts), (VEC[:, 0:len(names)], d["vecs"]), (WK[:, :], d["wk"]), (WQV[:, :], d["wqv"]),
                 (WO0[:, :], d["wo0"]), (FW0[:, :], d["ffw0"]), (w3(FW1[:, :], a=4), d["ffw1"]),
                 (BIG1[:, 0:P], d["inpx"]), (WX1[:, :], d["inpx1"]), (TC2[:, :], d["tc2"]), (WZ2[:, :], d["inpz"]),
                 (TAP2[:, :], d["cw2"].partition_broadcast(P)), (WO2[:, :], d["wo2"]),
                 (DTW2[96:96 + RANK, :], d["dtw2"]), (DTB2[:, :], d["dtb2"]), (AN2[:, :], d["al2"]),
                 (TAP3[:, :], d["dw3"].partition_broadcast(P)), (WU3, d["inpu3"]), (WZ3[:, :], d["inpz3"]),
                 (TAPU3[:, :], d["cw3"].partition_broadcast(P)), (DTW3[96:96 + RANK, :], d["dtw3"]),
                 (DTB3[:, :], d["dtb3"]), (AN3[:, :], d["al3"]), (WO3[:, :], d["wo3"]), (XP3[:, 96:104], d["xdt3"])]
        LOADS += [(XP2v[:, :, :, 96:104], d["xdt2"])]
        LOADS += [(XP2v[:, :, :, 32 * r:32 * r + 32], d["xbc2"]) for r in range(3)]
        BLOCKS = [(t[32 * g:32 * g + 32, 32 * g:32 * g + 32], d[n][g]) for t, n in
                  ((BD1, "w1"), (W23, "w2"), (WOUT3, "wout")) for g in range(4)]
        BLOCKS += [(XP3[:, 32 * r:32 * r + 2 * SN3], d["xbc3"]) for r in range(3)]
        NLOADS = 16 * (len(LOADS) + len(BLOCKS))

        @block.sync
        def _(e):
            for dst, src in LOADS:
                e.dma_start(dst, src).then_inc(weights_in, 16)
            e.wait_ge(zeroed, 4)
            for dst, src in BLOCKS:
                e.dma_start(dst, src).then_inc(weights_in, 16)
            e.wait_ge(pe_setup, 1)
            with e.Fori(0, B) as b:
                e.dma_start(X[:, :], x_in[bass.ds(b, 1), :, :].rearrange("o p l -> (o p) l")).then_inc(x_loaded, 16)
                e.dma_start(BIG2[:, 0:L], d["spec1"]).then_inc(spec_loaded, 16)
                e.dma_start(BIG2[:, L:2 * L], d["spec2"]).then_inc(spec_loaded, 16)
                e.wait_ge(x_added, NCH * LAYERS)
                e.dma_start(out[bass.ds(b, 1), :, :].rearrange("o p l -> (o p) l"), X[:, :]).then_inc(x_stored, 16)
                e.wait_ge(x_stored, 16)
                e.wait_ge(sample_done, 4)
                for s in persistent + [sample_done]:
                    e.sem_clear(s)
                e.sem_inc(next_sample, 1)

        def meet(e, b):
            e.sem_inc(sample_done, 1)
            e.wait_ge(next_sample, b + 1)

        @block.gpsimd
        def _(e):
            for t in (BD1, W23, WOUT3):
                nc.gpsimd.memset(t[:, :], 0.0).then_inc(zeroed, 1)
            nc.gpsimd.memset(XP3[:, 0:96], 0.0).then_inc(zeroed, 1)

            def steps_of(S):
                w, N = S.halves, S.states

                def sum_dt(k, c, par, h):
                    after(e, S.dt_steps, 2 * w, k, c, 2 * h + 2)
                    after(e, S.softplus, 6 * w, k, c, 6 * h + 6)
                    dt = S.of(S.DT, c, par)[:, ch(h)]
                    nc.gpsimd.tensor_tensor(dt, dt, S.LE[:, ch(h)], ADD).then_inc(S.dt_made, 1)

                def make_du(k, c, par):
                    after(e, S.dt_made, w, k, c, w)
                    if not S.ahead:
                        after(e, S.drive, N, k, c, -N)
                    pos = S.position(k, c)
                    nc.gpsimd.tensor_tensor(S.like(S.of(S.DU, c, par), k), S.like(S.of(S.DT, c, par), k), S.cols(BIG1, S.u0, k, pos),
                                            MUL).then_inc(S.du_ready, 1)
                return sum_dt, make_du

            def scan(S):
                w, N = S.halves, S.states
                sum_dt, make_du = steps_of(S)

                def body(k, c, par, prv, nxt):
                    for n in range(N):
                        if n == 0:
                            after(e, S.du_ready, 1, k, c, 1)
                        after(e, S.b_copied, N, k, c, n + 1)
                        after(e, S.summed, N, k, c, n + 1 - S.back[n])
                        q = S.Bq[n].rearrange("p (d l) -> p d l", l=NT)
                        u = S.of(S.DU, c, par).rearrange("p (d l) -> p d l", l=NT)
                        nc.gpsimd.tensor_tensor(q, u, S.Bs[n % 4].unsqueeze(1).to_broadcast([P, w, NT]),
                                                MUL).then_inc(S.drive, 1)
                        if S.ahead or not nxt:
                            continue
                        if n in S.p_sum:
                            sum_dt(*nxt, 1 - par, S.p_sum.index(n))
                        if n == S.p_du:
                            make_du(*nxt, 1 - par)

                if not S.ahead:
                    for h in range(w):
                        sum_dt(0, 0, 0, h)
                    make_du(0, 0, 0)
                S.chunks(e, body)

            def frame(done):
                nc.gpsimd.memset(XN3[:, 0, :], 0.0).then_inc(frame_zero, 1)
                nc.gpsimd.memset(XN3[:, PW - 1, :], 0.0).then_inc(frame_zero, 1)
                edge = XN[:, PW - 1:PW - 1 + (PW - 1) * PW].rearrange("p (h w) -> p h w", w=PW)[:, :, 0:2]
                e.wait_ge(frame_zero, done + 2)
                nc.gpsimd.memset(edge, 0.0).then_inc(frame_zero, 1)

            with e.Fori(0, B) as b:
                if LAYERS > 2:
                    e.wait_ge(gn_stats, 3)
                    frame(0)
                    for edge in (PX3[:, 0, :], PX3[:, PW - 1, :], PX3[:, 1:PW - 1, 0:1], PX3[:, 1:PW - 1, PW - 1:PW]):
                        nc.gpsimd.memset(edge, 0.0).then_inc(px_frame, 1)
                    scan(S2)
                    e.wait_ge(S2.y_taken, KDIR * NCH)
                    frame(3)
                    for j in range(NCH):
                        e.wait_ge(y_norm, j + 1)
                        e.wait_ge(z_act, 2 * NCH)
                        nc.gpsimd.tensor_tensor(Y2[:, :, ch(j)], Y2[:, :, ch(j)], Z2[:, :, ch(j)], MUL).then_inc(y_gated, 1)
                if LAYERS > 3:
                    e.wait_ge(y_gated, NCH)
                    e.wait_ge(y_out, NCH)
                    nc.gpsimd.memset(X1[:, 0:2], 0.0).then_inc(pad3, 1)
                    sum_dt, make_du = steps_of(S3)
                    for c in range(NCH):
                        sum_dt(0, c, 0, 0)
                        make_du(0, c, 0)
                    scan(S3)
                    for j in range(NCH):
                        e.wait_ge(S3.y_taken, j + 1)
                        e.wait_ge(z3_act, NCH)
                        nc.gpsimd.tensor_tensor(Y3[:, ch(j)], Y3[:, ch(j)], Z3[:, ch(j)], MUL).then_inc(g3_gated, 1)
                    e.wait_ge(g3_gated, NCH)
                meet(e, b)

        @block.tensor
        def _(e):
            def mm(o, w, r, start=True, stop=True):
                return nc.tensor.matmul(o, w, r, start=start, stop=stop)

            def group_norm(layer):
                e.wait_ge(gn_stats, layer + 1)
                mm(bank(7)[:, 0:1], cst["grp"], SM[:, 0:1]).then_inc(gn_mean, 1)
                e.wait_ge(gn_var, layer + 1)
                mm(bank(7)[:, 1:2], cst["grp"], SM[:, 4:5]).then_inc(gn_gvar, 1)
                e.wait_ge(xn_ready, 2 * layer + 2)

            def tail(layer, project):
                base = NCH * min(layer, 2)

                def variance(j):
                    e.wait_ge(t_sq, base + j + 1)
                    if base + j >= 2:
                        e.wait_ge(t_rstd, base + j - 1)
                    mm(bank(2 + j % 2), cst["ones"], SQ[j % 2]).then_inc(t_var, 1)

                for j in range(NCH):
                    if base + j >= 2:
                        e.wait_ge(t_norm, base + j - 1)
                    project(j).then_inc(t_proj, 1)
                    if j:
                        variance(j - 1)
                variance(NCH - 1)

            def block0():
                for j in range(NCH):
                    if j >= 2:
                        e.wait_ge(k_copied, j - 1)
                    mm(bank(j % 2), WK[:, :], XNF[:, ch(j)]).then_inc(k_proj, 1)
                for g in range(2 * NCH):
                    if g >= 4:
                        e.wait_ge(v_copied, g - 3)
                        e.wait_ge(q_shifted, g - 3)
                    for i in range(2):
                        r = mm(bank(2 + g % 4)[:, 256 * i:256 * (i + 1)], XNF[:, ch(2 * g + i, P)], WQV[:, :])
                    r.then_inc(qv_proj, 1)
                e.wait_ge(k_exp, 1)
                e.wait_ge(v_copied, 2 * NCH)

                def context(g):
                    e.wait_ge(kT_copied, g + 1)
                    for t in range(4 * g, 4 * g + 4):
                        r = mm(bank(6)[:, 0:P], VT[:, ch(t, P)], KT[:, ch(t, P)], t == 0, t == L // P - 1)
                    return r
                for g in range(NCH):
                    if g >= 2:
                        e.wait_ge(kT_copied, g - 1)
                    for i in range(4):
                        r = nc.tensor.transpose(bank(g % 2)[:, ch(i, P)], KC[:, ch(4 * g + i, P)], EYE)
                    r.then_inc(kT_made, 1)
                    if g:
                        context(g - 1)
                context(NCH - 1).then_inc(ctx_made, 1)
                for g in range(NCH):
                    e.wait_ge(q_norm, g // 2 + 1)
                    if g >= 2:
                        e.wait_ge(qT_copied, g - 1)
                    for i in range(4):
                        r = nc.tensor.transpose(bank(2 + g % 2)[:, ch(i, P)], QT[:, ch(4 * g + i, P)], EYE)
                    r.then_inc(qT_made, 1)
                e.wait_ge(ctx_masked, 1)
                mm(bank(6)[:, P:2 * P], CT, WO0[:, :]).then_inc(m2_made, 1)
                e.wait_ge(m2_ready, 1)
                e.wait_ge(qT_copied, NCH)
                tail(0, lambda j: mm(bank(j % 2), M2S, QC[:, ch(j)]))

            def block1():
                e.wait_ge(spec_loaded, 32)
                for x in range(2):
                    fwd = cst["fw" if x == 0 else "fh"]

                    def spectrum(g):
                        c = NCH * x + g
                        e.wait_ge(f_transc, c + 1)
                        if c // 2 >= 2 and g % 2 == 0:
                            e.wait_ge(f_specn, c // 2 - 1)
                            e.wait_ge(f_specp, 2 * (c // 2 - 1))
                        for i in range(4):
                            r = mm(bank(2 + (g // 2) % 2)[:, 256 * (g % 2) + 64 * i:256 * (g % 2) + 64 * (i + 1)],
                                   XT[g % 2][:, ch(i, P)], fwd)
                        if g % 2:
                            r.then_inc(f_spec, 1)

                    for g in range(NCH):
                        c = NCH * x + g
                        if c >= 2:
                            e.wait_ge(f_transc, c - 1)
                        for i in range(4):
                            t = 4 * g + i
                            tile = XNF[:, ch(t, P)] if x == 0 else XNF[:, t:L:HW // 2]
                            r = nc.tensor.transpose(bank(g % 2)[:, ch(i, P)], tile, EYE)
                        r.then_inc(f_trans, 1)
                        if g:
                            spectrum(g - 1)
                    spectrum(NCH - 1)
                for x in range(2):
                    for q in range(4):
                        c = 4 * x + q
                        e.wait_ge(f_specn, 4 * x + 4)
                        e.wait_ge(f_specp, 2 * (4 * x + 4))
                        if c >= 2:
                            e.wait_ge(f_mixc, c - 1)
                        for i in range(4):
                            y = 4 * q + i
                            o = bank(4 + q % 2)[:, ch(i, P)]
                            mm(o, SPEC[:, x, y, 0, :], S1[x][:, y, 1:3, :].rearrange("p b m -> p (b m)"), True, False)
                            r = mm(o, SPEC[:, x, y, 1, :], S1[x][:, y, 0:2, :].rearrange("p b m -> p (b m)"), False, True)
                        r.then_inc(f_mix, 1)
                for x in range(2):
                    for q in range(4):
                        c = 4 * x + q
                        e.wait_ge(f_mixc, 4 * x + 4)
                        if c >= 2:
                            e.wait_ge(f_mixTc, c - 1)
                        for i in range(4):
                            r = nc.tensor.transpose(bank(q % 2)[:, ch(i, P)], FS[x][:, ch(4 * q + i, P)], EYE)
                        r.then_inc(f_mixT, 1)
                for x in range(2):
                    for j in range(NCH):
                        c = NCH * x + j
                        e.wait_ge(f_mixTc, 4 * x + j // 2 + 1)
                        if c >= 2:
                            e.wait_ge(f_sum, c - 1)
                        for i in range(2):
                            r = mm(bank(2 + j % 2)[:, 256 * i:256 * (i + 1)], FT[x][:, ch(2 * j + i, P)], cst["fi"])
                        r.then_inc(f_inv, 1)
                e.wait_ge(f_sum, 2 * NCH)

                def hidden(j):
                    for f in range(4):
                        if j:
                            e.wait_ge((h_reluA, h_reluV)[f // 2], 2 * (j - 1) + f % 2 + 1)
                        mm(bank(4 + f), FW0[:, ch(f, P)], HF[:, ch(j)]).then_inc(h_proj, 1)

                def project(j):
                    if j == 0:
                        hidden(0)
                    if j + 1 < NCH:
                        hidden(j + 1)
                    e.wait_ge(h_reluA, 2 * j + 2)
                    e.wait_ge(h_reluV, 2 * j + 2)
                    for f in range(4):
                        r = mm(bank(j % 2), FW1[:, ch(f, P)], H1[j % 2][:, ch(f)], f == 0, f == 3)
                    return r
                tail(1, project)

            def steps_of(S):
                w, N = S.halves, S.states

                def rows(k, c, h):
                    if h == 0:
                        after(e, S.split_rest, 2, k, c, 0)
                        if w == 2:
                            after(e, S.softplus, 6 * w, k, c, 0)
                    src = S.cols(BIG1, S.u0, k, S.position(k, c))
                    wt = S.XP[:, 104 * (w * k + h):104 * (w * k + h + 1)]
                    mm(S.like(bank(6), k)[0:104, 0] if k % 2 else bank(6)[0:104, :], wt, src[:, h], h == 0, h == w - 1)\
                        .then_inc(S.rows_ready, 1)

                def steps(k, c, h):
                    after(e, S.split_cast, 4, k, c, 2)
                    if h == 0:
                        after(e, S.softplus, 6 * w, k, c, 0)
                    else:
                        after(e, S.split_rest, 2, k, c, 1)
                    mm(bank(7 - h), S.DTW[96:96 + RANK, P * (w * k + h):P * (w * k + h + 1)], S.R[96:96 + RANK, :])\
                        .then_inc(S.dt_raw, 1)
                return rows, steps

            def scan(S):
                w, N = S.halves, S.states
                rows, steps = steps_of(S)

                def bcast_b(k, c, par, n):
                    after(e, S.split_cast, 4, k, c, 4)
                    after(e, S.b_copied, N, k, c, n - 1)
                    mm(bank(4 + n % 2), SEL[0:96, ch(n, P)], S.of(S.TB, c, par)[0:96, :]).then_inc(S.b_bcast, 1)

                def bcast_c(k, c, par, n):
                    after(e, S.split_cast, 4, k, c, 4)
                    after(e, S.weighed, N, k, c, n - 1)
                    mm(bank(2 + n % 2), SEL[0:96, ch(N + n, P)], S.of(S.TB, c, par)[0:96, :]).then_inc(S.c_bcast, 1)

                def body(k, c, par, prv, nxt):
                    for n in range(N):
                        for f, ahead in ((bcast_b, 5), (bcast_c, 2)):
                            if n + ahead < N:
                                f(k, c, par, n + ahead)
                            elif nxt:
                                f(*nxt, 1 - par, n + ahead - N)
                        after(e, S.weighed, N, k, c, n + 1)
                        if n == 0:
                            after(e, S.y_taken, 1, k, c, 0)
                        for h in range(w):
                            r = mm(bank(h), EYE, S.Bq[n][:, ch(h)], n == 0, n == N - 1)
                        r.then_inc(S.summed, 1)
                        if S.ahead or not nxt:
                            continue
                        if 0 <= n - S.p_xp < w:
                            rows(*nxt, n - S.p_xp)
                        if 0 <= n - S.p_dt < w:
                            steps(*nxt, n - S.p_dt)

                if not S.ahead:
                    for h in range(w):
                        rows(0, 0, h)
                    for h in range(w):
                        steps(0, 0, h)
                bcast_b(0, 0, 0, 0)
                bcast_b(0, 0, 0, 1)
                bcast_c(0, 0, 0, 0)
                bcast_c(0, 0, 0, 1)
                bcast_b(0, 0, 0, 2)
                bcast_b(0, 0, 0, 3)
                bcast_b(0, 0, 0, 4)
                S.chunks(e, body)

            def block2():
                e.wait_ge(frame_zero, 3)
                for j in range(NCH):
                    if j >= 2:
                        e.wait_ge(px_copied, j - 1)
                    mm(bank(4 + j % 2), WX1[:, :], xn_mid(j)).then_inc(px_made, 1)
                for j in range(NCH):
                    if j >= 4:
                        e.wait_ge(conv_act, j - 3)
                    for t in range(9):
                        r = mm(bank(j % 4), TAP2[:, ch(t, P)], xn_tap(j, t), t == 0, t == 8)
                    r.then_inc(conv_done, 1)
                e.wait_ge(conv_act, NCH)
                e.wait_ge(dw_act, NCH)
                scan(S2)
                e.wait_ge(S2.y_taken, KDIR * NCH)
                for j in range(NCH):
                    for h in range(2):
                        c = 2 * j + h
                        if c >= 2:
                            e.wait_ge(z_act, c - 1)
                        e.wait_ge(xn_again, 1 + j // 4)
                        mm(bank(4 + h), WZ2[:, ch(h, P)], xn_mid(j)).then_inc(z_proj, 1)

                def mean(j):
                    if j >= 2:
                        e.wait_ge(y_cent, j - 1)
                    mm(bank(j % 2), cst["ones"], Y2[:, 0, ch(j)], True, False)
                    mm(bank(j % 2), cst["ones"], Y2[:, 1, ch(j)], False, True).then_inc(y_mean, 1)

                def variance(j):
                    e.wait_ge(y_sq, j + 1)
                    if j >= 2:
                        e.wait_ge(y_rstd, j - 1)
                    mm(bank(2 + j % 2), cst["ones"], Q2[j % 2][:, 0, :], True, False)
                    mm(bank(2 + j % 2), cst["ones"], Q2[j % 2][:, 1, :], False, True).then_inc(y_var, 1)

                def project(j):
                    e.wait_ge(y_gated, j + 1)
                    if j >= 2:
                        e.wait_ge(x_added, 2 * NCH + j - 1)
                    mm(bank(6 + j % 2), WO2[:, 0:P], Y2[:, 0, ch(j)], True, False)
                    mm(bank(6 + j % 2), WO2[:, P:2 * P], Y2[:, 1, ch(j)], False, True).then_inc(y_out, 1)
                mean(0)
                for j in range(NCH):
                    if j + 1 < NCH:
                        mean(j + 1)
                    variance(j)
                    if j:
                        project(j - 1)
                project(NCH - 1)

            def block3():
                e.wait_ge(frame_zero, 6)
                rows, steps = steps_of(S3)

                def taps(j, some):
                    if j >= 2 and some[0] == 0:
                        e.wait_ge(c3_act, j - 1)
                    for t in some:
                        r = mm(bank(j % 2), TAP3[:, ch(t, P)], xn_tap(j, t), t == 0, t == 8)
                    return r

                e.wait_ge(pad3, 1)
                todo = []
                for group in GROUPS3:
                    if todo:
                        todo.pop(0)()
                    for j in group:
                        taps(j, range(0, 5))
                        if todo:
                            todo.pop(0)()
                        taps(j, range(5, 9)).then_inc(c3_done, 1)
                        if todo:
                            todo.pop(0)()
                    while todo:
                        todo.pop(0)()
                    for j in group:
                        e.wait_ge(c3_act, j + 1)
                        if j >= 2:
                            e.wait_ge(u3_act, j - 1)
                        for t in range(3):
                            r = mm(bank(2 + j % 2), TAPU3[:, ch(t, P)], X1[:, NT * j + t:NT * j + t + NT], t == 0, t == 2)
                        r.then_inc(u3_proj, 1)
                        if j >= 2:
                            e.wait_ge(z3_act, j - 1)
                        mm(bank(4 + j % 2), WZ3[:, :], X1[:, NT * j + 2:NT * j + 2 + NT]).then_inc(z3_proj, 1)
                    for j in group:
                        todo += [lambda j=j: (e.wait_ge(u3_act, j + 1), rows(0, j, 0)), lambda j=j: steps(0, j, 0)]
                todo.pop(0)()
                for j in range(NCH):
                    e.wait_ge(z3_act, NCH if j < 2 else NCH + j - 1)
                    mm(bank(4 + j % 2), W23[:, :], xn_mid(j)).then_inc(z3_proj, 1)
                while todo:
                    todo.pop(0)()
                e.wait_ge(z3_act, 2 * NCH)
                scan(S3)

                def project(j):
                    e.wait_ge(g3_gated, j + 1)
                    return mm(bank(j % 2), WO3[:, :], Y3[:, ch(j)])
                e.wait_ge(S3.y_taken, NCH)
                tail(2, project)
                for j in range(NCH):
                    e.wait_ge(g3_fused, j + 1)
                    if j >= 2:
                        e.wait_ge(x_added, 3 * NCH + j - 1)
                    mm(bank(4 + j % 2), WOUT3[:, :], Y3[:, ch(j)]).then_inc(g3_out, 1)

            e.wait_ge(weights_in, NLOADS)
            e.wait_ge(vec_setup, 1)
            mm(bank(7)[:, 0:1], cst["cen"], vec["b_out"])
            mm(bank(7)[:, 1:2], cst["cen"], vec["ffb1"]).then_inc(pe_setup, 1)
            e.wait_ge(vec_ready, 1)
            with e.Fori(0, B) as b:
                for layer, run in enumerate((block0, block1, block2, block3)[:LAYERS]):
                    group_norm(layer)
                    run()
                meet(e, b)

        @block.scalar
        def _(e):
            chain = [0]
            chain_sem = [act_setup]

            def act(o, i, f, **k):
                return nc.scalar.activation(o, i, f, **k)

            def link(ins):
                chain[0] += 1
                ins.then_inc(chain_sem[0], 1)
                e.wait_ge(chain_sem[0], chain[0])

            def group_norm(layer):
                e.wait_ge(gn_gvar, layer + 1)
                link(act(SM[:, 6:7], bank(7)[:, 1:2], ACT.Ln, bias=vec["eps"]))
                act(SM[:, 7:8], SM[:, 6:7], ACT.Exp, scale=-0.5).then_inc(gn_rstd, 1)

            def tail(layer, bias):
                base = NCH * layer

                def rstd(j):
                    e.wait_ge(t_var, base + j + 1)
                    if base + j:
                        e.wait_ge(t_rstd, base + j)
                    link(act(LV, bank(2 + j % 2), ACT.Ln, bias=vec["eps"]))
                    if j >= 2:
                        e.wait_ge(x_added, base + j - 1)
                    act(RS[j % 2], LV, ACT.Exp, scale=-0.5).then_inc(t_rstd, 1)
                for j in range(NCH):
                    e.wait_ge(t_proj, base + j + 1)
                    if j >= 2:
                        e.wait_ge(t_var, base + j - 1)
                    act(SQ[j % 2], bank(j % 2), ACT.Square, bias=bias).then_inc(t_sq, 1)
                    if j:
                        rstd(j - 1)
                rstd(NCH - 1)

            def block0():
                for j in range(NCH):
                    e.wait_ge(k_proj, j + 1)
                    act(KC[:, ch(j)], bank(j % 2), ACT.Copy).then_inc(k_copied, 1)
                for g in range(2 * NCH):
                    e.wait_ge(q_shifted, g + 1)
                    act(w3(VT[:, ch(g, 256)], a=2), w3(bank(2 + g % 4), a=2)[:, :, P:2 * P], ACT.Copy).then_inc(v_copied, 1)
                e.wait_ge(k_shift, 1)
                e.wait_ge(k_copied, NCH)
                act(KC, KC, ACT.Exp, bias=KMX[:, 9:10], accum_out=KMX[:, 10:11]).then_inc(k_exp, 1)
                for i in range(4):
                    e.wait_ge(q_shifted, 4 * i + 4)
                    act(QT[:, ch(i, 1024)], QT[:, ch(i, 1024)], ACT.Exp).then_inc(q_exp, 1)
                for g in range(NCH):
                    e.wait_ge(qT_made, g + 1)
                    act(QC[:, ch(g)], bank(2 + g % 2), ACT.Copy).then_inc(qT_copied, 1)
                tail(0, vec["b_out_c"])

            def block1():
                def spectra(x, q):
                    c = 4 * x + q
                    e.wait_ge(f_specp, 2 * c + 2)
                    ps = bank(2 + q % 2).rearrange("p (t y i r) -> p i y t r", t=8, i=2, r=2)[:, 1]
                    o = S1[x][:, :, 0, :]
                    if x == 0:
                        o = o.rearrange("p y (t r) -> p y t r", r=2)[:, :, 8 * q:8 * q + 8, :]
                    else:
                        o = o.rearrange("p y (r t) -> p y t r", r=2)[:, :, 8 * q:8 * q + 8, :]
                    act(o, ps, ACT.Copy, scale=-1.0).then_inc(f_specn, 1)
                for x in range(2):
                    for q in range(4):
                        spectra(x, q)
                for x in range(2):
                    for q in range(4):
                        c = 4 * x + q
                        e.wait_ge(f_mix, c + 1)
                        o = FS[x].rearrange("p (m y) -> p y m", y=2 * MODES)[:, 8 * q:8 * q + 8, :]
                        act(o, w3(bank(4 + q % 2), a=8), ACT.Copy).then_inc(f_mixc, 1)
                for x in range(2):
                    for q in range(4):
                        e.wait_ge(f_mixT, 4 * x + q + 1)
                        act(FT[x][:, ch(q)], bank(q % 2), ACT.Copy).then_inc(f_mixTc, 1)

                def relu(j):
                    for f in range(2):
                        e.wait_ge(h_proj, 4 * j + f + 1)
                        if j >= 2:
                            e.wait_ge(t_proj, NCH + j - 1)
                        act(H1[j % 2][:, ch(f)], bank(4 + f), ACT.Relu, bias=vec[f"ffb0_{f}"]).then_inc(h_reluA, 1)
                base = NCH

                def square(j):
                    e.wait_ge(t_proj, base + j + 1)
                    if j >= 2:
                        e.wait_ge(t_var, base + j - 1)
                    act(SQ[j % 2], bank(j % 2), ACT.Square, bias=vec["ffb1_c"]).then_inc(t_sq, 1)

                def rstd(j):
                    e.wait_ge(t_var, base + j + 1)
                    if base + j:
                        e.wait_ge(t_rstd, base + j)
                    link(act(LV, bank(2 + j % 2), ACT.Ln, bias=vec["eps"]))
                    if j >= 2:
                        e.wait_ge(x_added, base + j - 1)
                    act(RS[j % 2], LV, ACT.Exp, scale=-0.5).then_inc(t_rstd, 1)
                relu(0)
                for j in range(NCH):
                    if j + 1 < NCH:
                        relu(j + 1)
                    square(j)
                    if j:
                        rstd(j - 1)
                rstd(NCH - 1)

            def steps_of(S):
                w, N = S.halves, S.states

                def split(k, c, par, part):
                    if part == 0:
                        after(e, S.rows_ready, w, k, c, w)
                        if not S.ahead:
                            after(e, S.b_bcast, N, k, c, -N)
                            after(e, S.c_bcast, N, k, c, -N)
                        act(S.of(S.TB, c, par)[0:96, :], bank(6)[0:96, :], ACT.Copy).then_inc(S.split_cast, 1)
                        act(S.R[96:96 + RANK, :], bank(6)[96:96 + RANK, :], ACT.Copy).then_inc(S.split_cast, 1)
                    else:
                        after(e, S.split_rest, 2, k, c, part)
                        act(S.of(S.TB, c, par)[0:96, :], S.R[0:96, :], ACT.Copy).then_inc(S.split_cast, 1)

                def softplus(k, c, par, h, part):
                    own = lambda i: after(e, S.softplus, 6 * w, k, c, 6 * h + i)
                    bias = S.DTB[:, w * k + h:w * k + h + 1]
                    if part == 0:
                        after(e, S.dt_raw, w, k, c, h + 1)
                        after(e, S.dt_steps, 2 * w, k, c, 2 * h)
                        act(S.TA, bank(7 - h), ACT.Abs, bias=bias).then_inc(S.softplus, 1)
                        own(1)
                        act(S.E, S.TA, ACT.Exp, scale=-1.0).then_inc(S.softplus, 1)
                    elif part == 1:
                        own(2)
                        act(S.TA, S.E, ACT.Square, bias=vec["series"], scale=3 ** -0.5).then_inc(S.softplus, 1)
                        act(S.MK, S.E, ACT.Relu, bias=vec["edge"], scale=-1.0).then_inc(S.softplus, 1)
                    else:
                        after(e, S.dt_made, w, k, c, 0)
                        act(S.LE[:, ch(h)], S.E, ACT.Ln, bias=vec["one"]).then_inc(S.softplus, 1)
                        if not S.ahead:
                            after(e, S.decay, N, k, c, -N)
                            after(e, S.du_ready, 1, k, c, -1)
                        act(S.of(S.DT, c, par)[:, ch(h)], bank(7 - h), ACT.Relu, bias=bias).then_inc(S.softplus, 1)
                return split, softplus

            def scan(S):
                w, N = S.halves, S.states
                split, softplus = steps_of(S)

                def copy_b(k, c, n):
                    after(e, S.b_bcast, N, k, c, n + 1)
                    after(e, S.drive, N, k, c, n - 3)
                    act(S.Bs[n % 4], bank(4 + n % 2), ACT.Copy).then_inc(S.b_copied, 1)

                def body(k, c, par, prv, nxt):
                    for n in range(N):
                        if n + 2 < N:
                            copy_b(k, c, n + 2)
                        elif nxt:
                            copy_b(*nxt, n + 2 - N)
                        if nxt and not S.ahead and n in (S.p_c1, S.p_c2, S.p_c3):
                            split(*nxt, 1 - par, (S.p_c1, S.p_c2, S.p_c3).index(n))
                        if n == 0:
                            after(e, S.dt_made, w, k, c, w)
                        after(e, S.scanned, N, k, c, n - 3)
                        for h in range(w):
                            col = (w * k + h) * N + n
                            r = act(S.A[n % 4][:, ch(h)], S.of(S.DT, c, par)[:, ch(h)], ACT.Exp, scale=S.AN[:, col:col + 1])
                        r.then_inc(S.decay, 1)
                        for h, start in enumerate(() if S.ahead else S.p_sp):
                            if nxt and 0 <= n - start < 3:
                                softplus(*nxt, 1 - par, h, n - start)

                if not S.ahead:
                    for part in range(3):
                        split(0, 0, 0, part)
                    for h in range(w):
                        for part in range(3):
                            softplus(0, 0, 0, h, part)
                copy_b(0, 0, 0)
                copy_b(0, 0, 1)
                S.chunks(e, body)

            def exp_and_log():
                e.preload_act_table_set("natural_log_exp_and_others")

            def block2():
                for j in range(NCH):
                    e.wait_ge(px_made, j + 1)
                    act(PX3[:, 1 + ROWS * j:1 + ROWS * (j + 1), 1:1 + HW], w3(bank(4 + j % 2), a=ROWS),
                        ACT.Copy).then_inc(px_copied, 1)
                for j in range(NCH):
                    e.wait_ge(dw_done, j + 1)
                    act(BIG1[:, L + j * NT:L + (j + 1) * NT], DW[j % 2], ACT.Silu, bias=vec["cb1"]).then_inc(dw_act, 1)
                    e.wait_ge(conv_done, j + 1)
                    act(BIG1[:, ch(j)], bank(j % 4), ACT.Silu, bias=vec["cb0"]).then_inc(conv_act, 1)
                exp_and_log()
                e.wait_ge(conv_act, NCH)
                e.wait_ge(dw_act, NCH)
                scan(S2)
                e.wait_ge(S2.du_ready, KDIR * NCH)
                for j in range(NCH):
                    for h in range(2):
                        e.wait_ge(z_proj, 2 * j + h + 1)
                        act(Z2[:, h, ch(j)], bank(4 + h), ACT.Silu).then_inc(z_act, 1)
                exp_and_log()

                def square(j):
                    e.wait_ge(y_cent, j + 1)
                    if j >= 2:
                        e.wait_ge(y_var, j - 1)
                    act(Q2[j % 2], Y2[:, :, ch(j)], ACT.Square).then_inc(y_sq, 1)

                def rstd(j):
                    e.wait_ge(y_var, j + 1)
                    if j:
                        e.wait_ge(y_rstd, j)
                    link(act(LV2, bank(2 + j % 2), ACT.Ln, bias=vec["eps"], scale=0.5))
                    if j >= 2:
                        e.wait_ge(y_norm, j - 1)
                    act(R2[j % 2], LV2, ACT.Exp, scale=-0.5).then_inc(y_rstd, 1)
                square(0)
                for j in range(NCH):
                    if j + 1 < NCH:
                        square(j + 1)
                    rstd(j)

            def block3():
                split, softplus = steps_of(S3)

                def steps(group):
                    for j in group:
                        for part in range(3):
                            split(0, j, 0, part)
                            if j > group[0]:
                                softplus(0, j - 1, 0, 0, part)
                    for part in range(3):
                        softplus(0, group[-1], 0, 0, part)
                for group in GROUPS3:
                    for j in group:
                        e.wait_ge(c3_done, j + 1)
                        act(X1[:, 2 + j * NT:2 + (j + 1) * NT], bank(j % 2), ACT.Silu).then_inc(c3_act, 1)
                    for j in group:
                        e.wait_ge(u3_proj, j + 1)
                        act(U3[:, ch(j)], bank(2 + j % 2), ACT.Silu, bias=vec["cb3"]).then_inc(u3_act, 1)
                        e.wait_ge(z3_proj, j + 1)
                        act(Z3[:, ch(j)], bank(4 + j % 2), ACT.Silu).then_inc(z3_act, 1)
                    if group[-1] < NCH - 1:
                        exp_and_log()
                        steps(group)
                for j in range(NCH):
                    e.wait_ge(z3_proj, NCH + j + 1)
                    act(X2G[:, ch(j)], bank(4 + j % 2), ACT.Silu).then_inc(z3_act, 1)
                exp_and_log()
                steps(GROUPS3[-1])
                scan(S3)

                base = 2 * NCH

                def rstd(j):
                    e.wait_ge(t_var, base + j + 1)
                    if base + j:
                        e.wait_ge(t_rstd, base + j)
                    link(act(LV, bank(2 + j % 2), ACT.Ln, bias=vec["eps"]))
                    if j >= 2:
                        e.wait_ge(g3_fused, j - 1)
                    act(RS[j % 2], LV, ACT.Exp, scale=-0.5).then_inc(t_rstd, 1)
                for j in range(NCH):
                    e.wait_ge(t_proj, base + j + 1)
                    if j >= 2:
                        e.wait_ge(t_var, base + j - 1)
                    act(SQ[j % 2], bank(j % 2), ACT.Square).then_inc(t_sq, 1)
                    if j:
                        rstd(j - 1)
                rstd(NCH - 1)

            exp_and_log()
            e.wait_ge(weights_in, NLOADS)
            for t in (AN2, AN3):
                link(act(t[:, :], t[:, :], ACT.Exp))
                link(act(t[:, :], t[:, :], ACT.Copy, scale=-1.0))
            with e.Fori(0, B) as b:
                chain[0], chain_sem[0] = 0, act_chain
                for layer, run in enumerate((block0, block1, block2, block3)[:LAYERS]):
                    group_norm(layer)
                    run()
                e.wait_ge(t_rstd, 8)
                meet(e, b)

        @block.vector
        def _(e):
            chain = [0]
            chain_sem = [vec_setup]
            V = nc.vector

            def link(ins):
                chain[0] += 1
                ins.then_inc(chain_sem[0], 1)
                e.wait_ge(chain_sem[0], chain[0])

            def group_norm(layer):
                if layer == 0:
                    e.wait_ge(x_loaded, 16)
                else:
                    e.wait_ge(x_added, NCH * layer)
                for j in range(NCH):
                    r = V.bn_stats(GST[:, 6 * j:6 * j + 6], X[:, ch(j)])
                link(r)
                V.bn_aggr(SM[:, 0:2], GST[:, :]).then_inc(gn_stats, 1)
                e.wait_ge(gn_mean, layer + 1)
                link(V.tensor_copy(SM[:, 5:6], bank(7)[:, 0:1]))
                link(V.tensor_sub(SM[:, 2:3], SM[:, 0:1], SM[:, 5:6]))
                link(V.tensor_tensor(SM[:, 3:4], SM[:, 2:3], SM[:, 2:3], MUL))
                V.tensor_tensor(SM[:, 4:5], SM[:, 3:4], SM[:, 1:2], ADD).then_inc(gn_var, 1)
                e.wait_ge(gn_rstd, layer + 1)
                link(V.tensor_tensor(SM[:, 8:9], SM[:, 5:6], SM[:, 7:8], MUL))
                normalise(layer, xn_ready)

            def normalise(layer, signal):
                for h in range(2):
                    o, i = XNF[:, ch(h, L // 2)], X[:, ch(h, L // 2)]
                    if layer >= 2:
                        o = XN3[:, 1 + 32 * h:33 + 32 * h, 1:1 + HW]
                        i = i.rearrange("p (h w) -> p h w", w=HW)
                    V.tensor_scalar(o, i, SM[:, 7:8], SM[:, 8:9], MUL, SUB).then_inc(signal, 1)

            def tail(layer, bias, g, b):
                for j in range(NCH):
                    e.wait_ge(t_rstd, NCH * layer + j + 1)
                    t = RS[j % 2]
                    V.scalar_tensor_tensor(t, bank(j % 2), bias, t, ADD, MUL).then_inc(t_norm, 1)
                    e.wait_ge(t_norm, NCH * layer + j + 1)
                    link(V.tensor_scalar(t, t, g, b, MUL, ADD))
                    V.tensor_tensor(X[:, ch(j)], X[:, ch(j)], t, ADD).then_inc(x_added, 1)

            def block0():
                for j in range(NCH):
                    e.wait_ge(k_copied, j + 1)
                    V.reduce_max(KMX[:, j:j + 1], KC[:, ch(j)], AXX).then_inc(k_max, 1)
                e.wait_ge(k_max, NCH)
                link(V.reduce_max(KMX[:, 8:9], KMX[:, 0:8], AXX))
                V.tensor_scalar(KMX[:, 9:10], KMX[:, 8:9], -1.0, None, MUL).then_inc(k_shift, 1)
                for g in range(2 * NCH):
                    e.wait_ge(qv_proj, g + 1)
                    q = bank(2 + g % 4).rearrange("p (t c) -> p t c", t=2)[:, :, 0:P].rearrange("p t (h d) -> p t h d", d=DH)
                    m = QMX[:, 8 * g:8 * g + 8].rearrange("p (t h) -> p t h", t=2)
                    link(V.reduce_max(m, q, AXX))
                    V.tensor_tensor(QT[:, ch(g, 256)].rearrange("p (t h d) -> p t h d", t=2, d=DH), q,
                                    m.unsqueeze(3).to_broadcast([P, 2, HEADS, DH]), SUB).then_inc(q_shifted, 1)
                for i in range(4):
                    e.wait_ge(q_exp, i + 1)
                    q = QT[:, ch(i, 1024)].rearrange("p (a d) -> p a d", d=DH)
                    s = QS[:, ch(i, 32)]
                    link(V.reduce_sum(s, q, AXX))
                    link(V.reciprocal(s, s))
                    V.tensor_tensor(q, q, s.unsqueeze(2).to_broadcast([P, 32, DH]), MUL).then_inc(q_norm, 1)
                for g in range(NCH):
                    e.wait_ge(kT_made, g + 1)
                    V.tensor_copy(KT[:, ch(g)], bank(g % 2)).then_inc(kT_copied, 1)
                e.wait_ge(ctx_made, 1)
                V.tensor_tensor(CT, bank(6)[:, 0:P], cst["head"], MUL).then_inc(ctx_masked, 1)
                e.wait_ge(k_exp, 1)
                link(V.reciprocal(KMX[:, 11:12], KMX[:, 10:11]))
                e.wait_ge(m2_made, 1)
                V.tensor_scalar(M2S, bank(6)[:, P:2 * P], KMX[:, 11:12], float(DH) ** -0.5, MUL, MUL).then_inc(m2_ready, 1)
                tail(0, vec["b_out_c"], vec["g0"], vec["b0"])

            def block1():
                for x in range(2):
                    def spectra(q):
                        c = 4 * x + q
                        e.wait_ge(f_spec, c + 1)
                        for im in range(2):
                            ps = bank(2 + q % 2).rearrange("p (t y i r) -> p i y t r", t=8, i=2, r=2)[:, im]
                            o = S1[x][:, :, 1 + im, :]
                            if x == 0:
                                o = o.rearrange("p y (t r) -> p y t r", r=2)[:, :, 8 * q:8 * q + 8, :]
                            else:
                                o = o.rearrange("p y (r t) -> p y t r", r=2)[:, :, 8 * q:8 * q + 8, :]
                            V.tensor_copy(o, ps).then_inc(f_specp, 1)
                    for g in range(NCH):
                        c = NCH * x + g
                        e.wait_ge(f_trans, c + 1)
                        V.tensor_copy(XT[g % 2], bank(g % 2)).then_inc(f_transc, 1)
                        if g % 2 == 0 and g:
                            spectra(g // 2 - 1)
                    spectra(3)
                for x in range(2):
                    for j in range(NCH):
                        e.wait_ge(f_inv, NCH * x + j + 1)
                        if x == 0:
                            V.tensor_copy(HF[:, ch(j)], bank(2 + j % 2)).then_inc(f_sum, 1)
                        else:
                            if j == 0:
                                e.wait_ge(f_sum, NCH)
                            h = HF.rearrange("p (m n) -> p n m", n=HW)[:, ROWS * j:ROWS * (j + 1), :]
                            V.tensor_tensor(h, h, w3(bank(2 + j % 2), a=ROWS), ADD).then_inc(f_sum, 1)

                def relu(j):
                    for f in range(2, 4):
                        e.wait_ge(h_proj, 4 * j + f + 1)
                        if j >= 2:
                            e.wait_ge(t_proj, NCH + j - 1)
                        V.tensor_scalar(H1[j % 2][:, ch(f)], bank(4 + f), vec[f"ffb0_{f}"], 0.0, ADD, MAX).then_inc(h_reluV, 1)
                relu(0)
                for j in range(NCH):
                    if j + 1 < NCH:
                        relu(j + 1)
                    e.wait_ge(t_rstd, NCH + j + 1)
                    t = RS[j % 2]
                    V.scalar_tensor_tensor(t, bank(j % 2), vec["ffb1_c"], t, ADD, MUL).then_inc(t_norm, 1)
                    e.wait_ge(t_norm, NCH + j + 1)
                    link(V.tensor_scalar(t, t, vec["g1"], vec["b1"], MUL, ADD))
                    V.tensor_tensor(X[:, ch(j)], X[:, ch(j)], t, ADD).then_inc(x_added, 1)

            def steps_of(S):
                w, N = S.halves, S.states

                def rest(k, c, par, part):
                    after(e, S.split_cast, 4, k, c, 3 if part else 1)
                    src = bank(6)[0:96, :] if part == 0 else S.R[0:96, :]
                    V.scalar_tensor_tensor(S.R[0:96, :], S.of(S.TB, c, par)[0:96, :], cst["m1" if part == 0 else "m2"][0:96, :],
                                           src, MUL, ADD).then_inc(S.split_rest, 1)

                def log_small(k, c, h):
                    after(e, S.softplus, 6 * w, k, c, 6 * h + 5)
                    V.scalar_tensor_tensor(S.TA, S.TA, 13.0 / 16, S.E, ADD, MUL).then_inc(S.dt_steps, 1)
                    after(e, S.dt_steps, 2 * w, k, c, 2 * h + 1)
                    V.memset(SM[:, 12:13], 0.0)
                    V.copy_predicated(S.LE[:, ch(h)], S.MK.bitcast(mybir.dt.uint32), S.TA).then_inc(S.dt_steps, 1)
                return rest, log_small

            def scan(S):
                w, N = S.halves, S.states
                rest, log_small = steps_of(S)

                def take_y(k, c):
                    after(e, S.summed, N, k, c, N)
                    pos = S.position(k, c)
                    y = S.cols(BIG2, S.y0, k, pos)
                    if k == 0:
                        u = S.cols(BIG1, S.u0, k, pos)
                        for h in range(w):
                            dd = vec[f"Dt{h}" if w == 2 else "Dp3"]
                            r = V.scalar_tensor_tensor(y[:, h], u[:, h], dd, bank(h), MUL, ADD)
                        r.then_inc(S.y_taken, 1)
                    else:
                        if k == 1:
                            after(e, S.y_taken, 1, k, 0, 0)
                        ps = PS[:, 0:w, :]
                        if k % 2:
                            ps = ps.rearrange("p d (w h) -> p d w h", h=HW)
                        V.tensor_tensor(y, y, ps, ADD).then_inc(S.y_taken, 1)

                def states(k, c, n):
                    after(e, S.decay, N, k, c, n + 1)
                    after(e, S.drive, N, k, c, n + 1)
                    after(e, S.carried, N, k, c, n + 1 - N)
                    q = S.Bq[n]
                    for h in range(w):
                        a, b = S.A[n % 4][:, ch(h)], q[:, ch(h)]
                        if k >= 2:
                            a, b = a[:, ::-1], b[:, ::-1]
                        first = k == 0 and isinstance(c, int) and c == 0
                        r = V.tensor_tensor_scan(b, a, b, 0.0 if first else S.HST[:, w * n + h:w * n + h + 1], MUL, ADD)
                    r.then_inc(S.scanned, 1)

                def body(k, c, par, prv, nxt):
                    rev = k >= 2
                    for n in range(N):
                        q = S.Bq[n]
                        after(e, S.scanned, N, k, c, n + 1)
                        last = 0 if rev else NT - 1
                        ends = q.rearrange("p (d l) -> p d l", l=NT)[:, :, last]
                        if isinstance(c, int) and c == NCH - 1:
                            V.memset(S.HST[:, w * n:w * n + w], 0.0).then_inc(S.carried, 1)
                        else:
                            V.tensor_copy(S.HST[:, w * n:w * n + w], ends).then_inc(S.carried, 1)
                        if n + 1 < N:
                            states(k, c, n + 1)
                        elif nxt:
                            states(*nxt, 0)
                        after(e, S.c_bcast, N, k, c, n + 1)
                        after(e, S.carried, N, k, c, n + 1)
                        qv = q.rearrange("p (d l) -> p d l", l=NT)
                        V.tensor_tensor(qv, qv, bank(2 + n % 2).unsqueeze(1).to_broadcast([P, w, NT]), MUL)\
                            .then_inc(S.weighed, 1)
                        if n == 0 and prv:
                            take_y(*prv)
                        if S.ahead or not nxt:
                            continue
                        if n == S.p_r1:
                            rest(*nxt, 1 - par, 0)
                        if n == S.p_r2:
                            rest(*nxt, 1 - par, 1)
                        if n in S.p_cb:
                            log_small(*nxt, S.p_cb.index(n))

                if not S.ahead:
                    rest(0, 0, 0, 0)
                    rest(0, 0, 0, 1)
                    for h in range(w):
                        log_small(0, 0, h)
                states(0, 0, 0)
                S.chunks(e, body)
                take_y(S.dirs - 1, NCH - 1)

            def block2():
                e.wait_ge(px_frame, 4)
                for j in range(NCH):
                    e.wait_ge(px_copied, min(j + 2, NCH))
                    if j >= 2:
                        e.wait_ge(dw_act, j - 1)
                    o = w3(DW[j % 2], a=ROWS)
                    for t in range(9):
                        r = ROWS * j + t // 3
                        i = PX3[:, r:r + ROWS, t % 3:t % 3 + HW]
                        if t == 0:
                            link(V.tensor_scalar(o, i, TC2[:, 0:1], None, MUL))
                        elif t < 8:
                            link(V.scalar_tensor_tensor(o, i, TC2[:, t:t + 1], o, MUL, ADD))
                        else:
                            V.scalar_tensor_tensor(o, i, TC2[:, t:t + 1], o, MUL, ADD).then_inc(dw_done, 1)
                scan(S2)
                normalise(2, xn_again)
                e.wait_ge(S2.y_taken, KDIR * NCH)

                def centre(j):
                    e.wait_ge(y_mean, j + 1)
                    for h in range(2):
                        r = V.scalar_tensor_tensor(Y2[:, h, ch(j)], bank(j % 2), -0.5, Y2[:, h, ch(j)], MUL, ADD)
                    r.then_inc(y_cent, 1)

                def add(j):
                    e.wait_ge(y_out, j + 1)
                    V.tensor_tensor(X[:, ch(j)], X[:, ch(j)], bank(6 + j % 2), ADD).then_inc(x_added, 1)
                centre(0)
                for j in range(NCH):
                    if j + 1 < NCH:
                        centre(j + 1)
                    e.wait_ge(y_rstd, j + 1)
                    e.wait_ge(y_sq, j + 1)
                    y = Y2[:, :, ch(j)]
                    link(V.tensor_tensor(y, y, R2[j % 2].unsqueeze(1).to_broadcast([P, 2, NT]), MUL))
                    for h in range(2):
                        r = V.tensor_scalar(Y2[:, h, ch(j)], Y2[:, h, ch(j)], vec[f"ng{h}"], vec[f"nb{h}"], MUL, ADD)
                    r.then_inc(y_norm, 1)
                    if j:
                        add(j - 1)
                add(NCH - 1)

            def block3():
                rest, log_small = steps_of(S3)
                for group in GROUPS3:
                    for j in group:
                        rest(0, j, 0, 0)
                        rest(0, j, 0, 1)
                        if j > group[0]:
                            log_small(0, j - 1, 0)
                    log_small(0, group[-1], 0)
                scan(S3)
                for j in range(NCH):
                    e.wait_ge(t_rstd, 2 * NCH + j + 1)
                    t = RS[j % 2]
                    V.tensor_tensor(t, bank(j % 2), t, MUL).then_inc(t_norm, 1)
                    e.wait_ge(t_norm, 2 * NCH + j + 1)
                    link(V.tensor_scalar(t, t, vec["gam3"], vec["bet3"], MUL, ADD))
                    e.wait_ge(z3_act, 2 * NCH)
                    V.tensor_tensor(Y3[:, ch(j)], t, X2G[:, ch(j)], MUL).then_inc(g3_fused, 1)
                for j in range(NCH):
                    e.wait_ge(g3_out, j + 1)
                    V.tensor_tensor(X[:, ch(j)], X[:, ch(j)], bank(4 + j % 2), ADD).then_inc(x_added, 1)

            e.wait_ge(weights_in, NLOADS)
            def centre_rows(t):
                link(V.reduce_sum(SM[:, 10:11], t, AXX))
                link(V.tensor_scalar(SM[:, 11:12], SM[:, 10:11], -1.0 / P, None, MUL))
                link(V.tensor_scalar(t, t, SM[:, 11:12], None, ADD))
            for t in [WO0[:, :], WO3[:, :]] + [FW1[:, ch(f, P)] for f in range(4)]:
                centre_rows(t)
            V.tensor_copy(w3(SEL[:, :], a=32), cst["onehot"].unsqueeze(2).to_broadcast([P, 32, P]))
            for h in range(2):
                link(V.tensor_tensor(vec[f"Dt{h}"], vec[f"D{h}"], vec[f"D{h + 2}"], ADD))
                link(V.tensor_tensor(vec[f"Dt{h}"], vec[f"Dt{h}"], vec[f"D{h + 4}"], ADD))
                link(V.tensor_tensor(vec[f"Dt{h}"], vec[f"Dt{h}"], vec[f"D{h + 6}"], ADD))
            for t, wt, n in ((TAP2, BIG1[:, 0:P], 9), (TAP3, BD1, 9), (TAPU3, WU3, 3)):
                wide = wt.unsqueeze(1).to_broadcast([P, n, wt.shape[1]])
                link(V.tensor_tensor(w3(t[:, :], a=n), w3(t[:, :], a=n), wide, MUL))
            e.wait_ge(pe_setup, 1)
            link(V.tensor_copy(vec["b_out_c"], bank(7)[:, 0:1]))
            V.tensor_copy(vec["ffb1_c"], bank(7)[:, 1:2]).then_inc(vec_ready, 1)
            e.wait_ge(vec_ready, 1)
            with e.Fori(0, B) as b:
                chain[0], chain_sem[0] = 0, dve_chain
                for layer, run in enumerate((block0, block1, block2, block3)[:LAYERS]):
                    group_norm(layer)
                    run()
                e.wait_ge(x_added, NCH * LAYERS)
                meet(e, b)


def kernel(**inputs):
    import concourse.bacc as _bacc
    from concourse.bass_utils import run_bass_kernel_spmd as _run

    a = {n: np.asarray(v) for n, v in inputs.items()}
    x = a["x"]
    B = x.shape[0]
    col = lambda v: v.reshape(P, 1)
    q, k, v = np.split(a["L0_conv_w_qkv"], 3, axis=1)
    Ds = a["L2_conv_Ds"].reshape(KDIR * 2, P)
    fill = lambda c: np.full((P, 1), c, np.float32)
    cols = [a["L0_conv_b_out"], fill(0), a["L0_conv_g_ln"], a["L0_conv_b_ln"], a["L1_conv_ff_b1"], fill(0),
            a["L1_conv_ln_g"], a["L1_conv_ln_b"], *a["L1_conv_ff_b0"].reshape(4, P),
            *a["L2_conv_conv_b"].reshape(2, P), *a["L2_conv_norm_g"].reshape(2, P), *a["L2_conv_norm_b"].reshape(2, P),
            *Ds, fill(0), fill(0), a["L3_conv_conv1d_b"], a["L3_conv_D_param"], a["L3_conv_gamma"], a["L3_conv_beta"],
            fill(1e-5), fill(1), fill(-0.75 * 3 ** -0.5), fill(1 / 128)]
    xp = a["L2_conv_x_proj_w"].reshape(KDIR, RANK + 2 * SN, 2, P).transpose(3, 0, 2, 1)
    xp3 = a["L3_conv_x_proj_w"].T
    ip2, ip3 = a["L2_conv_in_proj_w"].T, a["L3_conv_in_proj_w"].T
    halves = lambda w: w.reshape(*w.shape[:-1], 2, P)
    weights = {
        "vecs": np.concatenate([col(c) for c in cols], 1),
        "wk": k, "wqv": np.concatenate([q, v], 1), "wo0": a["L0_conv_w_out"],
        "spec1": a["L1_conv_w1"].transpose(0, 2, 3, 1).reshape(P, -1),
        "spec2": a["L1_conv_w2"].transpose(0, 2, 3, 1).reshape(P, -1),
        "ffw0": a["L1_conv_ff_w0"], "ffw1": a["L1_conv_ff_w1"].reshape(4, P, P).transpose(1, 0, 2),
        "inpx": ip2[:, :P], "inpx1": ip2[:, P:2 * P], "tc2": a["L2_conv_conv_w"].reshape(2 * P, 9)[P:], "inpz": ip2[:, 2 * P:],
        "cw2": a["L2_conv_conv_w"].reshape(2 * P, 9)[:P].T.reshape(-1),
        "wo2": a["L2_conv_out_proj_w"].T.reshape(2, P, P).transpose(1, 0, 2).reshape(P, -1),
        "dtw2": a["L2_conv_dt_proj_w"].transpose(2, 0, 1).reshape(RANK, -1),
        "dtb2": a["L2_conv_dt_proj_b"].reshape(KDIR * 2, P).T,
        "al2": a["L2_conv_A_logs"].reshape(KDIR * 2, P, SN).transpose(1, 0, 2).reshape(P, -1),
        "xdt2": xp[..., :RANK], "xbc2": xp[..., RANK:],
        "dw3": a["L3_conv_dw"].reshape(-1), "inpu3": ip3[:, :P], "inpz3": ip3[:, P:],
        "cw3": a["L3_conv_conv1d_w"].T.reshape(-1), "dtw3": a["L3_conv_dt_proj_w"].T,
        "dtb3": col(a["L3_conv_dt_proj_b"]), "al3": a["L3_conv_A_log"], "wo3": a["L3_conv_out_proj_w"].T,
        "xdt3": xp3[:, :RANK], "xbc3": xp3[:, RANK:],
        "w1": a["L3_conv_w1"].transpose(0, 2, 1), "w2": a["L3_conv_w2"].transpose(0, 2, 1),
        "wout": a["L3_conv_wout"].transpose(0, 2, 1),
    }
    nc = _bacc.Bacc("TRN2", target_bir_lowering=False, num_devices=1)
    arrays, handles = {}, {}
    sources = {"x": x.reshape(B, L, P).transpose(0, 2, 1), "consts": shape_constants(), **weights}
    for name, value in sources.items():
        value = np.ascontiguousarray(value)
        arrays[f"in_{name}_dram"] = value
        handles[name] = nc.dram_tensor(f"in_{name}_dram", value.shape, mybir.dt.from_np(value.dtype), kind="ExternalInput").ap()
    out = nc.dram_tensor("out_0_dram", (B, P, L), mybir.dt.float32, kind="ExternalOutput").ap()
    program(nc, handles["x"], handles["consts"], {n: handles[n] for n in weights}, out)
    r = _run(nc, [arrays], core_ids=[0])
    return np.ascontiguousarray(r.results[0]["out_0_dram"].transpose(0, 2, 1)).reshape(x.shape)
```
